# Optimizing a Trainium2 kernel written in Bass

```python
import numpy as np
import jax
import jax.numpy as jnp

def _softmax(x, axis=-1):
    return jax.nn.softmax(x, axis=axis)

def _gelu(x):
    return jax.nn.gelu(x, approximate=True)

def _silu(x):
    return jax.nn.silu(x)

def _sigmoid(x):
    return jax.nn.sigmoid(x)

def _layernorm(x, axis=-1, eps=1e-05):
    m = jnp.mean(x, axis=axis, keepdims=True)
    v = jnp.var(x, axis=axis, keepdims=True)
    return (x - m) / jnp.sqrt(v + eps)

def _scatter_add(tgt, idx, src, axis=0):
    return tgt.at[idx].add(src)

def _segment_sum(src, seg, n):
    return jax.ops.segment_sum(src, seg, n)
kernel_name = 'mk_decoder_postln_d1_seqx_r4_112c3c'

def setup_inputs(seed: int=0):
    np.random.seed(seed)
    _w = jnp.asarray

    def _rec_inputs():
        import jax
        import jax.numpy as jnp
        _rk = jax.random.key(seed)
        x = 7.22e-05 + 1 * jax.random.normal(jax.random.fold_in(_rk, 1), (8, 512, 256), jnp.float32)
        _lenS = 512 - jax.random.randint(jax.random.fold_in(_rk, 7), (8,), 0, max(1, 512 // 4) + 1, jnp.int32)
        _lenS2 = 512 - jax.random.randint(jax.random.fold_in(_rk, 8), (8,), 0, max(1, 512 // 4) + 1, jnp.int32)
        _ctx_1024P = jax.random.normal(jax.random.fold_in(_rk, 11), (8, 16, 256), jnp.float32)
        _ctx_1024c = jax.random.dirichlet(jax.random.fold_in(_rk, 511), 0.3 * jnp.ones((16,), jnp.float32), (8, 512))
        _ctx_1024t = jnp.einsum('bsk,bkd->bsd', _ctx_1024c, _ctx_1024P)
        _ctx_1024t = _ctx_1024t * jax.lax.rsqrt(jnp.mean(jnp.square(_ctx_1024t)) + 1e-12) * 0.953939
        ctx_1024 = 4.13588e-05 + 0.999923 * (_ctx_1024t + 0.3 * jax.random.normal(jax.random.fold_in(_rk, 611), (8, 512, 256), jnp.float32))
        return (x, ctx_1024)
    x, ctx_1024 = _rec_inputs()

    def _L0_attn_setup():
        import jax, jax.numpy as jnp
        import numpy as np
        B, T, DIM = (2, 256, 256)
        H, D = (16, 64)
        key = jax.random.key(seed)
        k1, k2, k3, k4 = jax.random.split(key, 4)
        s = DIM ** (-0.5)
        return {'x': jax.random.normal(k1, (B, T, DIM), jnp.float32), 'w_qkv': jax.random.normal(k2, (DIM, 3 * H * D), jnp.float32) * s, 'w_gate': jax.random.normal(k3, (DIM, H * D), jnp.float32) * s, 'w_out': jax.random.normal(k4, (H * D, DIM), jnp.float32) * s}
    _L0_attn_all = _L0_attn_setup()
    _L0_attn_in = {k: v for k, v in _L0_attn_all.items() if k in ('w_qkv', 'w_gate', 'w_out')}
    del _L0_attn_all

    def _L0_xattn_setup():
        import jax, jax.numpy as jnp
        import numpy as np
        D_MODEL = 256
        NUM_HEADS = 16
        key = jax.random.key(seed)
        ks = jax.random.split(key, 11)
        B, T, D = (4, 512, D_MODEL)
        scale = 1.0 / np.sqrt(D)
        inp = {'q': jax.random.normal(ks[0], (B, T, D), jnp.float32), 'k': jax.random.normal(ks[1], (B, T, D), jnp.float32), 'v': jax.random.normal(ks[2], (B, T, D), jnp.float32), 'W_q': jax.random.normal(ks[3], (D, D), jnp.float32) * scale, 'b_q': jnp.zeros((D,), jnp.float32), 'W_k': jax.random.normal(ks[4], (D, D), jnp.float32) * scale, 'b_k': jnp.zeros((D,), jnp.float32), 'W_v': jax.random.normal(ks[5], (D, D), jnp.float32) * scale, 'b_v': jnp.zeros((D,), jnp.float32), 'W_o': jax.random.normal(ks[6], (D, D), jnp.float32) * scale, 'b_o': jnp.zeros((D,), jnp.float32)}
        return inp
    _L0_xattn_all = _L0_xattn_setup()
    _L0_xattn_in = {k: v for k, v in _L0_xattn_all.items() if k in ('W_q', 'b_q', 'W_k', 'b_k', 'W_v', 'b_v', 'W_o', 'b_o')}
    del _L0_xattn_all

    def _L0_ffn_setup():
        import jax, jax.numpy as jnp
        import numpy as np
        B, N, D = (4, 512, 256)
        SPARSITY = 0.01
        key = jax.random.key(seed)
        k1, k2, k3 = jax.random.split(key, 3)
        x = jax.random.normal(k1, (B, N, D), dtype=jnp.float32)
        spatial = jax.random.normal(k2, (D, D), dtype=jnp.float32) * 0.02
        freq = jnp.fft.fft(spatial, axis=-1)
        k = int(D * SPARSITY)
        mag = jnp.abs(freq)
        kth = jax.lax.top_k(mag, k)[0][:, -1:]
        w_sparse = jnp.where(mag >= kth, freq, 0.0 + 0j)
        bias = jax.random.normal(k3, (D,), dtype=jnp.float32) * 0.01
        return {'x': x, 'w_freq_real': jnp.real(w_sparse).astype(jnp.float32), 'w_freq_imag': jnp.imag(w_sparse).astype(jnp.float32), 'bias': bias}
    _L0_ffn_all = _L0_ffn_setup()
    _L0_ffn_in = {k: v for k, v in _L0_ffn_all.items() if k in ('w_freq_real', 'w_freq_imag', 'bias')}
    del _L0_ffn_all
    return {'x': x, 'ctx_1024': ctx_1024, 'L0_attn_w_qkv': _L0_attn_in['w_qkv'], 'L0_attn_w_gate': _L0_attn_in['w_gate'], 'L0_attn_w_out': _L0_attn_in['w_out'], 'L0_xattn_W_q': _L0_xattn_in['W_q'], 'L0_xattn_b_q': _L0_xattn_in['b_q'], 'L0_xattn_W_k': _L0_xattn_in['W_k'], 'L0_xattn_b_k': _L0_xattn_in['b_k'], 'L0_xattn_W_v': _L0_xattn_in['W_v'], 'L0_xattn_b_v': _L0_xattn_in['b_v'], 'L0_xattn_W_o': _L0_xattn_in['W_o'], 'L0_xattn_b_o': _L0_xattn_in['b_o'], 'L0_ffn_w_freq_real': _L0_ffn_in['w_freq_real'], 'L0_ffn_w_freq_imag': _L0_ffn_in['w_freq_imag'], 'L0_ffn_bias': _L0_ffn_in['bias']}

def reference(x, ctx_1024, L0_attn_w_qkv, L0_attn_w_gate, L0_attn_w_out, L0_xattn_W_q, L0_xattn_b_q, L0_xattn_W_k, L0_xattn_b_k, L0_xattn_W_v, L0_xattn_b_v, L0_xattn_W_o, L0_xattn_b_o, L0_ffn_w_freq_real, L0_ffn_w_freq_imag, L0_ffn_bias):
    import jax
    import jax.numpy as jnp

    def _L0_attn_ref(x, w_qkv, w_gate, w_out):
        import jax, jax.numpy as jnp
        import numpy as np
        B, T, DIM = (2, 256, 256)
        H, D = (16, 64)
        b, t, c = x.shape
        qkv = (x @ w_qkv).reshape(b, t, 3, H, D)
        q, k, v = (qkv[:, :, 0], qkv[:, :, 1], qkv[:, :, 2])
        gate = jax.nn.sigmoid((x @ w_gate).reshape(b, t, H, D))
        q = jax.nn.elu(q) + 1.0
        k = jax.nn.elu(k) + 1.0
        k_cum = jnp.cumsum(k, axis=1)
        kv = jnp.cumsum(k[..., None, :] * v[..., :, None], axis=1)
        numerator = jnp.einsum('bthj,bthij->bthi', q, kv)
        denominator = jnp.einsum('bthj,bthj->bth', q, k_cum)
        out = numerator / (denominator[..., None] + 1e-06)
        out = out * gate
        return out.reshape(b, t, H * D) @ w_out

    def _L0_xattn_ref(q, k, v, W_q, b_q, W_k, b_k, W_v, b_v, W_o, b_o):
        import jax, jax.numpy as jnp
        import numpy as np
        D_MODEL = 256
        NUM_HEADS = 16
        B, T, D = q.shape
        H = NUM_HEADS
        hd = D // H

        def split_heads(x):
            return x.reshape(B, T, H, hd).transpose(0, 2, 1, 3)
        qh = split_heads(q @ W_q + b_q)
        kh = split_heads(k @ W_k + b_k)
        vh = split_heads(v @ W_v + b_v)
        score = jnp.einsum('bhqd,bhkd->bhqk', qh, kh) / jnp.sqrt(jnp.float32(hd))
        attn = jax.nn.softmax(score, axis=-1)
        out = jnp.einsum('bhqk,bhkd->bhqd', attn, vh)
        out = out.transpose(0, 2, 1, 3).reshape(B, T, D)
        return out @ W_o + b_o

    def _L0_ffn_ref(x, w_freq_real, w_freq_imag, bias):
        import jax, jax.numpy as jnp
        import numpy as np
        B, N, D = (4, 512, 256)
        SPARSITY = 0.01
        w = jax.lax.complex(w_freq_real, w_freq_imag)
        x_freq = jnp.fft.fft(x, axis=-1)
        y_freq = jnp.einsum('bnd,do->bno', x_freq, w)
        y = jnp.real(jnp.fft.ifft(y_freq, axis=-1))
        return y + bias
    x = _layernorm(x + _L0_attn_ref(x, L0_attn_w_qkv, L0_attn_w_gate, L0_attn_w_out), axis=-1)
    x = _layernorm(x + _L0_xattn_ref(x, ctx_1024, ctx_1024, L0_xattn_W_q, L0_xattn_b_q, L0_xattn_W_k, L0_xattn_b_k, L0_xattn_W_v, L0_xattn_b_v, L0_xattn_W_o, L0_xattn_b_o), axis=-1)
    x = _layernorm(x + _L0_ffn_ref(x, L0_ffn_w_freq_real, L0_ffn_w_freq_imag, L0_ffn_bias), axis=-1)
    return x

_drawn_inputs = setup_inputs


def setup_inputs(seed=0):
    import zlib

    import numpy as np

    out = dict(_drawn_inputs(seed))
    spreads = {'L0_xattn_b_q': (0.0, 0.44),
     'L0_xattn_b_k': (0.0, 0.8),
     'L0_xattn_b_v': (0.0, 0.1),
     'L0_xattn_b_o': (0.0, 0.1)}
    factors = {'L0_ffn_bias': 6.943}
    for name, (base, spread) in spreads.items():
        noise = np.random.default_rng([zlib.crc32(name.encode()), seed]).standard_normal(out[name].shape)
        drawn = base * np.exp(spread * noise) if base else spread * noise
        out[name] = jnp.asarray(drawn.astype(out[name].dtype))
    for name, factor in factors.items():
        out[name] = (out[name] * factor).astype(out[name].dtype)
    return out
```

```python
from contextlib import ExitStack

import concourse.bass as bass
from concourse import mybir

ALU = mybir.AluOpType
ACT = mybir.ActivationFunctionType
F32 = mybir.dt.float32
F32R = mybir.dt.float32r
BF16 = mybir.dt.bfloat16
I32 = mybir.dt.int32
X = mybir.AxisListType.X

P = 128
EPS_LN = 1e-5
EPS_DEN = 1e-6
RSQRT_SEED = 0x5F3759DF
TERMS = [(0, 0), (0, 1), (1, 0), (0, 2), (2, 0), (1, 1)]


def decoder_kernel(nc, x, ctx, w_qkv, w_gate, w_out, W_q, b_q, W_k, b_k, W_v, b_v, W_o, b_o,
                   w_re, w_im, f_bias, consts, dft, out):
    B, T, C = x.shape
    H = 16
    D = w_gate.shape[1] // H
    HD = C // H
    NT = T // P
    NC = C // P
    PAIRS = H // 2
    V1 = D + 1
    QUERY_SCALE = float(HD) ** -0.5
    assert (T, C, D, HD) == (512, 256, 64, 16)

    with ExitStack() as stack:
        def sb(name, shape, dt=F32):
            return stack.enter_context(nc.sbuf_tensor(name, shape, dt))

        def sem(name):
            return stack.enter_context(nc.semaphore(name))

        wqk_hi, wqk_lo = (sb(n, [P, NC, 2 * H * D], F32R) for n in ("wqk_hi", "wqk_lo"))
        wvg_hi, wvg_lo = (sb(n, [P, NC, 4, 512], F32R) for n in ("wvg_hi", "wvg_lo"))
        wout_hi, wout_lo = (sb(n, [P, PAIRS, C], F32R) for n in ("wout_hi", "wout_lo"))
        wx_hi, wx_lo = (sb(n, [P, 4, NC, C], F32R) for n in ("wx_hi", "wx_lo"))
        mix_hi, mix_lo = (sb(n, [P, NC, C], F32R) for n in ("mix_hi", "mix_lo"))

        ident_mask = sb("ident_mask", [P, 2 * P])
        ident = ident_mask[:, 0:P]
        causal = ident_mask[:, P:2 * P]
        bv_rows, bo_rows, fb_rows = (sb(n, [P, C]) for n in ("bv_rows", "bo_rows", "fb_rows"))
        bq_col, bk_col, bqs_col = (sb(n, [P, NC]) for n in ("bq_col", "bk_col", "bqs_col"))

        land = sb("land", [P, NT, C])
        xw = sb("xw", [P, NT, C])
        ta_hi, ta_lo, tb_hi, tb_lo = (sb(n, [P, NC, T], F32R) for n in ("ta_hi", "ta_lo", "tb_hi", "tb_lo"))
        og_hi, og_lo = (sb(n, [P, 2, T], F32R) for n in ("og_hi", "og_lo"))
        v1 = sb("v1", [P, 2, NT, 4, V1])
        state = sb("state", [P, NT - 1, 2, V1])
        v2 = sb("v2", [P, NT, H, 32])
        ks = sb("ks", [98, H, T], BF16)
        mv = sb("mv", [P, NT, 2])
        bn6 = sb("bn6", [P, NT, 6])
        rs_v, rs_y, rs_t = (sb(n, [P, NT]) for n in ("rs_v", "rs_y", "rs_t"))
        den = sb("den", [P, 4])
        rden = sb("rden", [P, 4])
        rsum = sb("rsum", [P, NT, 4])
        negmax = sb("negmax", [P, 2, NT, 8])
        mrow_hi, mrow_lo = (sb(n, [8, T], BF16) for n in ("mrow_hi", "mrow_lo"))

        ARENA = 34 * 256
        arena = sb("arena", [P, ARENA])
        at = [0]

        def take(n, dt=F32):
            a = arena[:, at[0]:at[0] + n]
            at[0] += n
            assert at[0] <= ARENA
            return a if dt is F32 else a.bitcast(dt)

        raw = [take(2048) for _ in range(4)]
        at[0] = 0
        q1 = take(2 * T).rearrange("p (s t) -> p s t", s=2)
        k1 = take(2 * T).rearrange("p (s t) -> p s t", s=2)
        e_part = take(2 * T).rearrange("p (s t) -> p s t", s=2)
        r_part = take(2 * T).rearrange("p (s t) -> p s t", s=2)
        ktok = take(3 * P).rearrange("p (c j) -> p c j", c=3)
        gate = take(2 * NT * 256).rearrange("p (s t n) -> p s t n", s=2, t=NT)
        sT = take(2 * T).rearrange("p (h t) -> p h t", h=2)
        og = take(NT * P).rearrange("p (t n) -> p t n", t=NT)
        at[0] = 0
        qs = take(H * T // 2, BF16).rearrange("p (h t) -> p h t", h=H)
        at_probs = at[0]
        probs = take(2 * 4 * T).rearrange("p (s h t) -> p s h t", s=2, h=4)
        oT = take(T)
        at[0] = at_probs
        parts = take(4 * 3 * T // 2, BF16).rearrange("p (u k t) -> p u k t", u=4, k=3)
        rest = take(2 * T).rearrange("p (s t) -> p s t", s=2)

        staged_parts = nc.dram_tensor("staged_parts", [2, 2, P, 3, T], BF16).ap()

        T0, T1, PJ0, PJ1, S0, S1, OA, OB = BANKS = ["T0", "T1", "PJ0", "PJ1", "S0", "S1", "OA", "OB"]
        ps = {b: stack.enter_context(nc.psum_tensor("ps_" + b, [P, 512], F32)) for b in BANKS}
        TB, PJ, SB, OBANK, FOUR = [T0, T1], [PJ0, PJ1], [S0, S1], [OA, OB], [T0, T1, PJ0, PJ1]

        full_act = {b: sem("full_act_" + b) for b in FOUR}
        full_dve = {b: sem("full_dve_" + b) for b in [PJ0, PJ1, S0, S1, OA, OB]}
        handed = {b: sem("handed_" + b) for b in TB}
        evacuated = {b: sem("evacuated_" + b) for b in BANKS}
        elu_halves = sem("elu_halves")
        state_ready = sem("state_ready")
        og_ready = sem("og_ready")
        x1_ready = sem("x1_ready")
        x2_ready = sem("x2_ready")
        out_ready = sem("out_ready")
        stored = sem("stored")
        x_landed = sem("x_landed")
        ctx_landed = sem("ctx_landed")
        x_consumed = sem("x_consumed")
        att_consumed = sem("att_consumed")
        first_part = sem("first_part")
        parts_ready = sem("parts_ready")
        parts_staged = sem("parts_staged")
        stacked = [sem(f"stacked_{m}") for m in range(2)]
        mrow_first = sem("mrow_first")
        mrow_ready = sem("mrow_ready")
        mrow_landed = sem("mrow_landed")
        dve_done = sem("dve_done")
        raw_landed = [sem(f"raw_landed_{n}") for n in range(6)]
        w_hi_done = sem("w_hi_done")
        w_lo_done = sem("w_lo_done")
        consts_landed = sem("consts_landed")
        four_landed = sem("four_landed")
        spec_full = sem("spec_full")
        spec_copied = sem("spec_copied")
        mix_full = sem("mix_full")
        mix_hi_done = sem("mix_hi_done")
        filled = sem("filled")

        pieces = [
            (wqk_hi[:, :, 0:1024], wqk_lo[:, :, 0:1024]),
            (wqk_hi[:, :, 1024:2048], wqk_lo[:, :, 1024:2048]),
            (wvg_hi[:, :, :, 0:256], wvg_lo[:, :, :, 0:256]),
            (wvg_hi[:, :, :, 256:512], wvg_lo[:, :, :, 256:512]),
            (wout_hi[:], wout_lo[:]),
            (wx_hi[:], wx_lo[:]),
        ]

        def raw_view(n):
            r = raw[n % 4]
            if n < 2:
                return r.rearrange("p (k c) -> p k c", k=NC)
            if n < 4:
                return r.rearrange("p (k g c) -> p k g c", k=NC, g=4)
            if n == 4:
                return r.rearrange("p (k c) -> p k c", k=PAIRS)
            return r.rearrange("p (w k c) -> p w k c", w=4, k=NC)

        w_spec = xw[:].rearrange("p (s k) c -> p s k c", s=2)
        table = v2[:].rearrange("p a b c -> p (a b c)")[:, 0:3 * NC * C].rearrange("p (s k c) -> p s k c", s=3, k=NC)
        specT = land[:].rearrange("p (s k) c -> p s k c", s=2)

        block = stack.enter_context(nc.Block())

        @block.sync
        def _(sp):
            def tiles(w):
                return w.rearrange("(k p) c -> p k c", p=P)

            sources = [
                [(raw_view(0), tiles(w_qkv[:, 0:1024]))],
                [(raw_view(1), tiles(w_qkv[:, 1024:2048]))],
                [(raw[2].rearrange("p (k c) -> p k c", k=NC), tiles(w_qkv[:, 2048:3072]))],
                [(raw[3].rearrange("p (k c) -> p k c", k=NC), tiles(w_gate))],
                [(raw_view(4), tiles(w_out))],
                [(raw_view(5)[:, n], tiles(w)) for n, w in enumerate((W_q, W_k, W_v, W_o))],
            ]
            for n, loads in enumerate(sources):
                if n >= 4:
                    sp.wait_ge(w_hi_done, n - 3)
                    sp.wait_ge(w_lo_done, n - 3)
                for dst, src in loads:
                    sp.dma_start(dst, src).then_inc(raw_landed[n], 16)
                if n == 3:
                    sp.dma_start(w_spec[:, 0], tiles(w_re)).then_inc(four_landed, 16)
                    sp.dma_start(w_spec[:, 1], tiles(w_im)).then_inc(four_landed, 16)
                    sp.dma_start(table, dft.rearrange("s (k p) c -> p s k c", p=P)).then_inc(four_landed, 16)
                    sp.dma_start(ident_mask[:], consts).then_inc(consts_landed, 16)
                    for dst, src in ((bv_rows, b_v), (bo_rows, b_o), (fb_rows, f_bias)):
                        sp.dma_start(dst[:], src.partition_broadcast(P)).then_inc(consts_landed, 16)
                    for dst, src in ((bq_col, b_q), (bk_col, b_k)):
                        sp.dma_start(dst[:], src.rearrange("(m p) -> p m", p=P),
                                     allow_slow_non_contiguous=True).then_inc(consts_landed, 16)
            sp.wait_ge(mix_hi_done, 1)
            sp.dma_start(land[:], x[0].rearrange("(t p) c -> p t c", p=P)).then_inc(x_landed, 16)
            with sp.Fori(0, B) as b:
                sp.wait_ge(x_consumed, 1)
                sp.sem_inc(x_consumed, -1)
                sp.dma_start(land[:], ctx[bass.ds(b, 1)].rearrange("o (t p) c -> p (o t) c", p=P)).then_inc(ctx_landed, 16)

                def stage(side, m):
                    sp.wait_ge(parts_ready, 2 * side + m + 1)
                    sp.dma_start(staged_parts[side, m], parts[:, 2 * side + m]).then_inc(parts_staged, 16)

                def lay_out(side, m):
                    dst = (ks, qs)[side]
                    for n, term in enumerate(TERMS):
                        sp.dma_start(dst[HD * n:HD * (n + 1), 8 * m:8 * m + 8, :],
                                     staged_parts[side, m][:, term[side]].rearrange("(h d) t -> d h t", d=HD)
                                     ).then_inc(stacked[m], 16)

                stage(0, 0)
                stage(0, 1)
                sp.wait_ge(parts_staged, 32)
                lay_out(0, 0)
                lay_out(0, 1)
                for m in range(2):
                    stage(1, m)
                    sp.wait_ge(parts_staged, 48 + 16 * m)
                    lay_out(1, m)
                sp.sem_inc(parts_staged, -64)
                sp.sem_inc(parts_ready, -4)
                for m in range(2):
                    sp.wait_ge(mrow_ready, m + 1)
                    for row, src in ((96, mrow_hi), (97, mrow_lo)):
                        sp.dma_start(qs[row:row + 1, 8 * m:8 * m + 8, :], src[:]).then_inc(mrow_landed, 16)
                sp.sem_inc(mrow_ready, -2)
                sp.wait_ge(att_consumed, 1)
                sp.sem_inc(att_consumed, -1)
                sp.dma_start(land[:], x[bass.ds((b + 1) % B, 1)].rearrange("o (t p) c -> p (o t) c", p=P)).then_inc(x_landed, 16)
                sp.wait_ge(out_ready, 1)
                sp.sem_inc(out_ready, -1)
                sp.dma_start(out[bass.ds(b, 1)].rearrange("o (t p) c -> p (o t) c", p=P), xw[:]).then_inc(stored, 16)

        @block.gpsimd
        def _(pool):
            pool.memset(v1[:], 1.0).then_inc(filled, 1)
            pool.wait_ge(filled, 1)
            pool.memset(state[:], 0.0).then_inc(filled, 1)
            pool.wait_ge(filled, 2)
            pool.memset(ks[96:98], 1.0).then_inc(filled, 1)
            pool.wait_ge(filled, 3)
            pool.wait_ge(mix_hi_done, 1)
            pool.memset(v2[:, :, :, HD + 1:32], 0.0).then_inc(filled, 1)
            pool.wait_ge(filled, 4)
            pool.memset(v2[:, :, :, 0:HD + 1], 1.0).then_inc(filled, 1)

        @block.tensor
        def _(pe):
            pe.wait_ge(four_landed, 48)
            COS, SIN, NCOS = range(3)
            for s, (a, b) in enumerate(((COS, SIN), (SIN, NCOS))):
                for f in range(NC):
                    for e in range(NC):
                        for part, tab in enumerate((a, b)):
                            last = pe.matmul(ps[TB[s]][:, f * C:(f + 1) * C], w_spec[:, part, e, f * P:(f + 1) * P],
                                             table[:, tab, e, :], start=(f == e == part == 0),
                                             stop=(e == part == 1), skip_group_check=True)
                last.then_inc(spec_full, 1)
            pe.wait_ge(spec_copied, 2)
            for d in range(NC):
                for s, tab in enumerate((COS, SIN)):
                    for f in range(NC):
                        last = pe.matmul(ps[PJ0][:, d * C:(d + 1) * C], specT[:, s, f, d * P:(d + 1) * P],
                                         table[:, tab, f, :], start=(d == s == f == 0), stop=(s == f == 1),
                                         skip_group_check=True)
            last.then_inc(mix_full, 1)
            for bank in BANKS:
                pe.sem_inc(evacuated[bank], 1)
            pe.wait_ge(w_lo_done, 7)
            pe.wait_ge(consts_landed, 96)
            pe.wait_ge(filled, 5)

            with pe.Fori(0, B) as _b:
                uses = dict.fromkeys(BANKS, 0)

                def claim(bank):
                    uses[bank] += 1
                    pe.wait_ge(evacuated[bank], uses[bank])

                def evacuated_last(*banks):
                    for bank in banks:
                        pe.wait_ge(evacuated[bank], uses[bank] + 1)

                def three(out, lhs, rhs, start, stop):
                    for n, (i, j) in enumerate(((0, 0), (0, 1), (1, 0))):
                        last = pe.matmul(out, lhs[i], rhs[j], start=start and n == 0, stop=stop and n == 2,
                                         skip_group_check=True)
                    return last

                def turn(src, bank, c):
                    claim(bank)
                    for t in range(NT):
                        last = pe.transpose(ps[bank][:, t * P:(t + 1) * P], src[:, t, c * P:(c + 1) * P], ident)
                    last.then_inc(full_act[bank], 1)

                def project(bank, w, cols, a, done):
                    claim(bank)
                    for c in range(NC):
                        last = three(ps[bank][:], [w[0][:, c, cols], w[1][:, c, cols]], [a[0][:, c, :], a[1][:, c, :]],
                                     c == 0, c == NC - 1)
                    last.then_inc(done[bank], 1)

                def token_major(bank, u, a, w, depth):
                    claim(bank)
                    for i in range(2):
                        t = 2 * u + i
                        for c in range(depth):
                            last = three(ps[bank][:, i * C:(i + 1) * C],
                                         [a[0][:, c, t * P:(t + 1) * P], a[1][:, c, t * P:(t + 1) * P]],
                                         [w[0][:, c, :], w[1][:, c, :]], i == 0 and c == 0, c == depth - 1)
                    last.then_inc(full_dve[bank], 1)

                ta, tb, og_t = (ta_hi, ta_lo), (tb_hi, tb_lo), (og_hi, og_lo)
                wqk = (wqk_hi, wqk_lo)

                qk_use = {}

                def project_qk(p, side):
                    at_col = side * H * D + p * P
                    project(PJ[side], wqk, slice(at_col, at_col + P), ta, full_act)
                    qk_use[p, side] = uses[PJ[side]]

                def values_gate(g, t):
                    bank = PJ[t % 2]
                    claim(bank)
                    for c in range(NC):
                        last = three(ps[bank][:], [ta_hi[:, c, t * P:(t + 1) * P], ta_lo[:, c, t * P:(t + 1) * P]],
                                     [wvg_hi[:, c, g, :], wvg_lo[:, c, g, :]], c == 0, c == NC - 1)
                    last.then_inc(full_act[bank], 1)

                pe.wait_ge(x_landed, 16)
                pe.sem_inc(x_landed, -16)
                for c in range(NC):
                    turn(land, TB[c], c)
                evacuated_last(T0, T1)
                project_qk(0, 0)
                project_qk(0, 1)
                for t in range(NT):
                    values_gate(0, t)

                def out_project(g):
                    for u in range(2):
                        token_major(PJ[u], u, og_t, (wout_hi[:, 2 * g:2 * g + 2], wout_lo[:, 2 * g:2 * g + 2]), 2)

                def turn_og(p):
                    pe.wait_ge(og_ready, p + 1)
                    claim(T1)
                    for t in range(NT):
                        last = pe.transpose(ps[T1][:, t * P:(t + 1) * P], og[:, t, :], ident)
                    last.then_inc(full_act[T1], 1)

                def attend(p, c, bank, at0):
                    o = ps[bank][:, at0:at0 + 2 * V1]
                    ch = slice(c * P, (c + 1) * P)
                    if c > 0:
                        pe.matmul(o, q1[:, p % 2, ch], state[:, c - 1].rearrange("p h v -> p (h v)"),
                                  start=False, stop=False, skip_group_check=True)
                    for h in range(2):
                        last = pe.matmul(o[:, h * V1:(h + 1) * V1], sT[:, h, ch],
                                         v1[:, (p // 2) % 2, c, 2 * (p % 2) + h, :],
                                         start=(c == 0 and h == 0), stop=True, skip_group_check=True)
                    return last

                for p in range(PAIRS):
                    for side in range(2):
                        pe.wait_ge(evacuated[PJ[side]], qk_use[p, side] + 1)
                    claim(S0)
                    claim(S1)
                    for c in range(NT):
                        ch = slice(c * P, (c + 1) * P)
                        for h in range(2):
                            hd = slice(h * D, (h + 1) * D)
                            last = pe.matmul(ps[SB[h]][:, ch], k1[hd, p % 2, ch], q1[hd, p % 2, ch],
                                             start=True, stop=True)
                            if c == NT - 1:
                                last.then_inc(full_dve[SB[h]], 1)
                    if p + 1 < PAIRS:
                        project_qk(p + 1, 0)
                    claim(T0)
                    for c in range(NT - 1):
                        last = pe.transpose(ps[T0][:, c * P:(c + 1) * P], k1[:, p % 2, c * P:(c + 1) * P], ident)
                    last.then_inc(full_act[T0], 1)
                    if p + 1 < PAIRS:
                        project_qk(p + 1, 1)
                    claim(OB)
                    evacuated_last(T0)
                    for c in range(NT - 1):
                        for h in range(2):
                            last = pe.matmul(ps[OB][h * D:(h + 1) * D, c * V1:(c + 1) * V1], ktok[:, c, h * D:(h + 1) * D],
                                             v1[:, (p // 2) % 2, c, 2 * (p % 2) + h, :],
                                             start=(c == 0), stop=True, skip_group_check=True)
                    last.then_inc(full_dve[OB], 1)
                    if p >= 1:
                        turn_og(p - 1)
                    g_next = p // 2 + 1
                    if g_next < 4:
                        values_gate(g_next, 2 * (p % 2))
                    claim(OA)
                    evacuated_last(S0, S1)
                    attend(p, 0, OA, 0)
                    pe.wait_ge(state_ready, p + 1)
                    attend(p, 1, OA, 2 * V1).then_inc(full_dve[OA], 1)
                    if g_next < 4:
                        values_gate(g_next, 2 * (p % 2) + 1)
                    attend(p, 2, OB, 3 * V1)
                    attend(p, 3, OB, 5 * V1).then_inc(full_dve[OB], 1)
                    if p >= 2 and p % 2 == 0:
                        evacuated_last(T1)
                        out_project(p // 2 - 1)
                        if p == 2:
                            evacuated_last(PJ0, PJ1)
                            pe.sem_inc(x_consumed, 1)

                pe.wait_ge(ctx_landed, 16)
                pe.sem_inc(ctx_landed, -16)
                for c in range(NC):
                    turn(land, TB[c], c)
                turn_og(PAIRS - 1)
                evacuated_last(T0, T1)
                out_project(3)

                for m in range(2):
                    project(PJ[m], (wx_hi[:, 1], wx_lo[:, 1]), slice(m * P, (m + 1) * P), ta, full_act)
                for u in range(2):
                    token_major(PJ[u], u, ta, (wx_hi[:, 2], wx_lo[:, 2]), NC)
                pe.wait_ge(x1_ready, 1)
                for c in range(NC):
                    turn(xw, TB[c], c)
                evacuated_last(T0, T1)
                for m in range(2):
                    project(PJ[m], (wx_hi[:, 0], wx_lo[:, 0]), slice(m * P, (m + 1) * P), tb, full_act)

                def scores_by_query(h, t):
                    bank = SB[t % 2]
                    claim(bank)
                    pe.matmul(ps[bank][:], qs[0:96, h, t * P:(t + 1) * P], ks[0:96, h, :],
                              start=True, stop=True).then_inc(full_dve[bank], 1)

                def max_rows(m):
                    evacuated_last(S0, S1)
                    claim(PJ[m])
                    uses[PJ[m]] -= 1
                    for t in range(NT):
                        last = pe.matmul(ps[PJ[m]][0:8, t * P:(t + 1) * P], negmax[:, m, t, :], ident,
                                         start=True, stop=True)
                    last.then_inc(full_act[PJ[m]], 1)

                def scores_by_key(g, kt):
                    for j in range(4):
                        claim(FOUR[j])
                        pe.matmul(ps[FOUR[j]][:], ks[0:98, 4 * g + j, kt * P:(kt + 1) * P], qs[0:98, 4 * g + j, :],
                                  start=True, stop=True).then_inc(full_act[FOUR[j]], 1)

                def weigh(g, kt):
                    bank = OBANK[g % 2]
                    if kt == 0:
                        claim(bank)
                    for j in range(4):
                        last = pe.matmul(ps[bank][32 * j:32 * j + 32, :], v2[:, kt, 4 * g + j, :], probs[:, kt % 2, j, :],
                                         start=(kt == 0), stop=(kt == NT - 1), skip_group_check=True)
                    if kt == NT - 1:
                        last.then_inc(full_dve[bank], 1)

                def turn_back(g):
                    evacuated_last(OBANK[g % 2])
                    claim(S0)
                    for t in range(NT):
                        last = pe.transpose(ps[S0][:, t * P:(t + 1) * P], oT[:, t * P:(t + 1) * P], ident)
                    last.then_inc(full_dve[S0], 1)

                pe.wait_ge(stacked[0], 192)
                for h in range(8):
                    for t in range(NT):
                        scores_by_query(h, t)
                max_rows(0)
                pe.wait_ge(stacked[1], 192)
                pe.sem_inc(stacked[0], -192)
                pe.sem_inc(stacked[1], -192)
                steps = [(g, kt) for g in range(4) for kt in range(NT)]
                for n, (g, kt) in enumerate(steps):
                    if n == 0:
                        pe.wait_ge(mrow_landed, 32)
                    if n == 8:
                        max_rows(1)
                        evacuated_last(*FOUR)
                        weigh(*steps[n - 1])
                        pe.wait_ge(mrow_landed, 64)
                        pe.sem_inc(mrow_landed, -64)
                    scores_by_key(g, kt)
                    if n < 8:
                        for t in range(NT):
                            scores_by_query(8 + n, t)
                    if n >= 1 and n != 8:
                        weigh(*steps[n - 1])
                    if kt == 2 and g >= 1:
                        turn_back(g - 1)
                evacuated_last(*FOUR)
                weigh(*steps[-1])
                turn_back(3)
                evacuated_last(S0)
                for c in range(NC):
                    turn(land, TB[c], c)
                evacuated_last(T0, T1)
                pe.sem_inc(att_consumed, 1)
                for u in range(2):
                    token_major(PJ[u], u, tb, (wx_hi[:, 3], wx_lo[:, 3]), NC)

                pe.wait_ge(x2_ready, 1)
                for c in range(NC):
                    turn(xw, TB[c], c)
                evacuated_last(T0, T1)
                for u in range(2):
                    token_major(PJ[u], u, tb, (mix_hi, mix_lo), NC)

                for s, n in [(state_ready, PAIRS), (og_ready, PAIRS), (x1_ready, 1), (x2_ready, 1)] + [
                        (evacuated[bank], uses[bank]) for bank in BANKS]:
                    pe.wait_ge(s, n)
                    pe.sem_inc(s, -n)
            pe.wait_ge(x_landed, 16)

        @block.scalar
        def _(act):
            for n, (hi, _lo) in enumerate(pieces):
                act.wait_ge(raw_landed[n], 64 if n == 5 else 16)
                act.activation(hi, raw_view(n), ACT.Copy).then_inc(w_hi_done, 1)
            for s in range(2):
                act.wait_ge(spec_full, s + 1)
                act.activation(specT[:, s].rearrange("p k c -> p (k c)"), ps[TB[s]][:], ACT.Copy).then_inc(spec_copied, 1)
            act.wait_ge(mix_full, 1)
            act.activation(mix_hi[:].rearrange("p k c -> p (k c)"), ps[PJ0][:], ACT.Copy, scale=1.0 / C).then_inc(mix_hi_done, 1)
            act.wait_ge(consts_landed, 96)
            act.activation(bqs_col[:], bq_col[:], ACT.Copy, scale=QUERY_SCALE)
            act.wait_ge(filled, 5)

            with act.Fori(0, B) as _b:
                seen = dict.fromkeys(FOUR, 0)

                def full(bank):
                    seen[bank] += 1
                    act.wait_ge(full_act[bank], seen[bank])

                def high(bank, hi):
                    full(bank)
                    act.activation(hi, ps[bank][:], ACT.Copy).then_inc(handed[bank], 1)

                def elu(side):
                    full(PJ[side])
                    act.activation(e_part[:, side, :], ps[PJ[side]][:], ACT.Exp)
                    act.activation(r_part[:, side, :], ps[PJ[side]][:], ACT.Relu).then_inc(elu_halves, 1)

                def values_gate(g, t):
                    bank = PJ[t % 2]
                    full(bank)
                    act.activation(v1[:, g % 2, t, :, 0:D], ps[bank][:, 0:256].rearrange("p (h d) -> p h d", h=4), ACT.Copy)
                    act.activation(gate[:, g % 2, t, :], ps[bank][:, 256:512], ACT.Tanh, scale=0.5).then_inc(evacuated[bank], 1)

                for c in range(NC):
                    high(TB[c], ta_hi[:, c, :])
                elu(0)
                elu(1)
                for t in range(NT):
                    values_gate(0, t)
                for p in range(PAIRS):
                    if p + 1 < PAIRS:
                        elu(0)
                    full(T0)
                    act.activation(ktok.rearrange("p c j -> p (c j)"), ps[T0][:, 0:3 * P], ACT.Copy).then_inc(evacuated[T0], 1)
                    if p + 1 < PAIRS:
                        elu(1)
                    if p >= 1:
                        high(T1, og_hi[:, (p - 1) % 2, :])
                    if p // 2 + 1 < 4:
                        for i in range(2):
                            values_gate(p // 2 + 1, 2 * (p % 2) + i)
                for c in range(NC):
                    high(TB[c], ta_hi[:, c, :])
                high(T1, og_hi[:, 1, :])

                def first_of_three(side, m):
                    full(PJ[m])
                    bias = (bk_col, bqs_col)[side][:, m:m + 1]
                    scale = (1.0, QUERY_SCALE)[side]
                    act.activation(parts[:, 2 * side + m, 0, :], ps[PJ[m]][:], ACT.Identity, bias=bias, scale=scale)
                    act.activation(rest[:, m, :], ps[PJ[m]][:], ACT.Identity, bias=bias, scale=scale).then_inc(first_part, 1)
                    act.drain().then_inc(evacuated[PJ[m]], 1)

                for m in range(2):
                    first_of_three(0, m)
                for c in range(NC):
                    high(TB[c], tb_hi[:, c, :])
                for m in range(2):
                    first_of_three(1, m)

                def max_rows(m):
                    full(PJ[m])
                    act.activation(mrow_hi[:], ps[PJ[m]][0:8, :], ACT.Copy).then_inc(mrow_first, 1)

                max_rows(0)
                for n in range(16):
                    if n == 8:
                        max_rows(1)
                    for j in range(4):
                        full(FOUR[j])
                        act.activation(probs[:, n % 2, j, :], ps[FOUR[j]][:], ACT.Exp).then_inc(evacuated[FOUR[j]], 1)
                for _n in range(2):
                    for c in range(NC):
                        high(TB[c], tb_hi[:, c, :])
                for bank in FOUR:
                    act.wait_ge(full_act[bank], seen[bank])
                    act.sem_inc(full_act[bank], -seen[bank])

        @block.vector
        def _(dve):
            for n, (hi, lo) in enumerate(pieces):
                dve.wait_ge(w_hi_done, n + 1)
                dve.tensor_tensor(lo, raw_view(n), hi.bitcast(F32), ALU.subtract).then_inc(w_lo_done, 1)
            dve.wait_ge(mix_hi_done, 1)
            dve.scalar_tensor_tensor(mix_lo[:].rearrange("p k c -> p (k c)"), ps[PJ0][:], 1.0 / C,
                                     mix_hi[:].rearrange("p k c -> p (k c)").bitcast(F32), ALU.mult, ALU.subtract
                                     ).then_inc(w_lo_done, 1)
            dve.sem_inc(stored, 16)
            dve.wait_ge(consts_landed, 96)
            dve.wait_ge(filled, 5)

            with dve.Fori(0, B) as _b:
                seen = dict.fromkeys([*full_dve, *(("handed", b) for b in TB), "elu", "first", "mrow"], 0)
                own = [0]

                def after(ins):
                    own[0] += 1
                    ins.then_inc(dve_done, 1)
                    dve.wait_ge(dve_done, own[0])

                def full(bank):
                    seen[bank] += 1
                    dve.wait_ge(full_dve[bank], seen[bank])

                def low(bank, hi, lo):
                    seen["handed", bank] += 1
                    dve.wait_ge(handed[bank], seen["handed", bank])
                    dve.tensor_tensor(lo, ps[bank][:], hi.bitcast(F32), ALU.subtract).then_inc(evacuated[bank], 1)

                def elu(dst, side):
                    seen["elu"] += 1
                    dve.wait_ge(elu_halves, seen["elu"])
                    dve.scalar_tensor_tensor(dst, e_part[:, side, :], 1.0, r_part[:, side, :], ALU.min, ALU.add
                                             ).then_inc(evacuated[PJ[side]], 1)

                def gated(p, half, bank, at0):
                    full(bank)
                    o = ps[bank][:, at0:at0 + 4 * V1].rearrange("p (n v) -> p n v", n=4)
                    after(dve.tensor_scalar(den[:], o[:, :, D], 2.0, 2.0 * EPS_DEN, ALU.mult, ALU.add))
                    after(dve.reciprocal(rden[:], den[:]))
                    dst = og[:, 2 * half:2 * half + 2, :]
                    after(dve.tensor_tensor(dst.rearrange("p c (h d) -> p (c h) d", h=2), o[:, :, 0:D],
                                            rden[:].unsqueeze(2).to_broadcast([P, 4, D]), ALU.mult))
                    gt = gate[:, (p // 2) % 2, 2 * half:2 * half + 2, (p % 2) * P:(p % 2 + 1) * P]
                    return dve.scalar_tensor_tensor(dst, gt, 1.0, dst, ALU.add, ALU.mult)

                def add_projected(u, base, width=2):
                    full(PJ[u])
                    return dve.tensor_tensor(xw[:, 2 * u:2 * u + 2, :], ps[PJ[u]][:].rearrange("p (t c) -> p t c", t=2),
                                             base[:, 2 * u:2 * u + 2, :], ALU.add).then_inc(evacuated[PJ[u]], 1)

                def layer_norm():
                    for t in range(NT):
                        ins = dve.bn_stats(bn6[:, t, :], xw[:, t, :])
                    after(ins)
                    for t in range(NT):
                        ins = dve.bn_aggr(mv[:, t, :], bn6[:, t, :])
                    after(ins)
                    after(dve.tensor_scalar(rs_v[:], mv[:, :, 1], EPS_LN, None, ALU.add))
                    after(dve.tensor_scalar(rs_t[:].bitcast(I32), rs_v[:].bitcast(I32), 1, None, ALU.logical_shift_right))
                    after(dve.tensor_scalar(rs_y[:].bitcast(I32), rs_t[:].bitcast(I32), -1.0, float(RSQRT_SEED), ALU.mult, ALU.add))
                    for _n in range(3):
                        after(dve.tensor_tensor(rs_t[:], rs_y[:], rs_y[:], ALU.mult))
                        after(dve.tensor_tensor(rs_t[:], rs_t[:], rs_v[:], ALU.mult))
                        after(dve.tensor_scalar(rs_t[:], rs_t[:], -0.5, 1.5, ALU.mult, ALU.add))
                        after(dve.tensor_tensor(rs_y[:], rs_y[:], rs_t[:], ALU.mult))
                    for t in range(NT):
                        ins = dve.tensor_scalar(xw[:, t, :], xw[:, t, :], mv[:, t, 0:1], rs_y[:, t:t + 1],
                                                ALU.subtract, ALU.mult)
                    return ins

                for c in range(NC):
                    low(TB[c], ta_hi[:, c, :], ta_lo[:, c, :])
                elu(q1[:, 0, :], 0)
                elu(k1[:, 0, :], 1)
                for p in range(PAIRS):
                    for h in range(2):
                        full(SB[h])
                        dve.tensor_tensor(sT[:, h, :].rearrange("p (c t) -> p c t", c=NT),
                                          ps[SB[h]][:].rearrange("p (c t) -> p c t", c=NT),
                                          causal.unsqueeze(1).to_broadcast([P, NT, P]), ALU.mult
                                          ).then_inc(evacuated[SB[h]], 1)
                    if p + 1 < PAIRS:
                        elu(q1[:, (p + 1) % 2, :], 0)
                        elu(k1[:, (p + 1) % 2, :], 1)
                    full(OB)
                    for c in range(NT - 1):
                        for h in range(2):
                            hd = slice(h * D, (h + 1) * D)
                            src = ps[OB][hd, c * V1:(c + 1) * V1]
                            if c == 0:
                                ins = dve.tensor_copy(state[hd, c, h, :], src)
                            else:
                                ins = dve.tensor_tensor(state[hd, c, h, :], src, state[hd, c - 1, h, :], ALU.add)
                        if c < NT - 2:
                            after(ins)
                    ins.then_inc(state_ready, 1)
                    if p >= 1:
                        low(T1, og_hi[:, (p - 1) % 2, :], og_lo[:, (p - 1) % 2, :])
                    gated(p, 0, OA, 0).then_inc(evacuated[OA], 1)
                    gated(p, 1, OB, 3 * V1).then_inc(og_ready, 1)
                    dve.drain().then_inc(evacuated[OB], 1)
                    if p >= 2 and p % 2 == 0:
                        if p == 2:
                            dve.wait_ge(stored, 16)
                            dve.sem_inc(stored, -16)
                        for u in range(2):
                            add_projected(u, land if p == 2 else xw)
                for c in range(NC):
                    low(TB[c], ta_hi[:, c, :], ta_lo[:, c, :])
                low(T1, og_hi[:, 1, :], og_lo[:, 1, :])
                for u in range(2):
                    add_projected(u, xw)
                dve.drain().then_inc(dve_done, 1)
                own[0] += 1
                dve.wait_ge(dve_done, own[0])
                layer_norm().then_inc(x1_ready, 1)

                def parts_two_three(side, m):
                    seen["first"] += 1
                    dve.wait_ge(first_part, seen["first"])
                    three = parts[:, 2 * side + m]
                    r = rest[:, m, :]
                    after(dve.tensor_tensor(r, r, three[:, 0, :], ALU.subtract))
                    after(dve.tensor_copy(three[:, 1, :], r))
                    dve.tensor_tensor(three[:, 2, :], r, three[:, 1, :], ALU.subtract).then_inc(parts_ready, 1)

                for m in range(2):
                    parts_two_three(0, m)
                for u in range(2):
                    full(PJ[u])
                    for i in range(2):
                        ins = dve.tensor_tensor(v2[:, 2 * u + i, :, 0:HD],
                                                ps[PJ[u]][:, i * C:(i + 1) * C].rearrange("p (h d) -> p h d", h=H),
                                                bv_rows[:].rearrange("p (h d) -> p h d", h=H), ALU.add)
                    ins.then_inc(evacuated[PJ[u]], 1)
                for c in range(NC):
                    low(TB[c], tb_hi[:, c, :], tb_lo[:, c, :])
                for m in range(2):
                    parts_two_three(1, m)

                def add_rows(rows):
                    after(dve.tensor_tensor(xw[:], xw[:], rows[:].unsqueeze(1).to_broadcast([P, NT, C]), ALU.add))

                add_rows(bo_rows)

                def row_max(h, t):
                    bank = SB[t % 2]
                    full(bank)
                    dve.tensor_reduce(negmax[:, h // 8, t, h % 8:h % 8 + 1], ps[bank][:], X, ALU.max, negate=True
                                      ).then_inc(evacuated[bank], 1)

                def max_rows():
                    seen["mrow"] += 1
                    dve.wait_ge(mrow_first, seen["mrow"])
                    m = seen["mrow"] - 1
                    dve.tensor_tensor(mrow_lo[:], ps[PJ[m]][0:8, :], mrow_hi[:], ALU.subtract).then_inc(mrow_ready, 1)

                def keep_sums(g):
                    bank = OBANK[g % 2]
                    full(bank)
                    dve.tensor_copy(oT, ps[bank][:]).then_inc(evacuated[bank], 1)

                def normalise(g):
                    full(S0)
                    o = ps[S0][:].rearrange("p (t h d) -> p t h d", t=NT, h=4)
                    after(dve.reciprocal(rsum[:], o[:, :, :, HD]))
                    dst = land[:, :, g * 4 * HD:(g + 1) * 4 * HD].rearrange("p t (h d) -> p t h d", h=4)
                    dve.tensor_tensor(dst, o[:, :, :, 0:HD], rsum[:].unsqueeze(3).to_broadcast([P, NT, 4, HD]), ALU.mult
                                      ).then_inc(evacuated[S0], 1)

                for h in range(8):
                    for t in range(NT):
                        row_max(h, t)
                max_rows()
                for n in range(16):
                    if n < 8:
                        for t in range(NT):
                            row_max(8 + n, t)
                    if n == 7:
                        max_rows()
                    if n % 4 == 0 and n > 0:
                        keep_sums(n // 4 - 1)
                    if n % 4 == 2 and n > 2:
                        normalise(n // 4 - 1)
                keep_sums(3)
                normalise(3)
                for c in range(NC):
                    low(TB[c], tb_hi[:, c, :], tb_lo[:, c, :])
                for u in range(2):
                    add_projected(u, xw)
                dve.drain().then_inc(dve_done, 1)
                own[0] += 1
                dve.wait_ge(dve_done, own[0])
                layer_norm().then_inc(x2_ready, 1)
                for c in range(NC):
                    low(TB[c], tb_hi[:, c, :], tb_lo[:, c, :])
                add_rows(fb_rows)
                for u in range(2):
                    add_projected(u, xw)
                dve.drain().then_inc(dve_done, 1)
                own[0] += 1
                dve.wait_ge(dve_done, own[0])
                layer_norm().then_inc(out_ready, 1)

                for s, n in [(full_dve[b], seen[b]) for b in full_dve] + [(handed[b], seen["handed", b]) for b in TB] + [
                        (elu_halves, seen["elu"]), (first_part, seen["first"]), (mrow_first, seen["mrow"]),
                        (dve_done, own[0])]:
                    dve.wait_ge(s, n)
                    dve.sem_inc(s, -n)
            dve.wait_ge(stored, 16)


_INS = ['x', 'ctx_1024', 'L0_attn_w_qkv', 'L0_attn_w_gate', 'L0_attn_w_out', 'L0_xattn_W_q', 'L0_xattn_b_q',
        'L0_xattn_W_k', 'L0_xattn_b_k', 'L0_xattn_W_v', 'L0_xattn_b_v', 'L0_xattn_W_o', 'L0_xattn_b_o',
        'L0_ffn_w_freq_real', 'L0_ffn_w_freq_imag', 'L0_ffn_bias']


def kernel(**inputs):
    import numpy as np
    import concourse.bacc as bacc
    from concourse.bass_utils import run_bass_kernel_spmd

    nc = bacc.Bacc("TRN2", target_bir_lowering=False, num_devices=1)
    arrays, args = {}, []

    def give(name, a):
        a = np.ascontiguousarray(a)
        arrays[name] = a
        args.append(nc.dram_tensor(name, a.shape, mybir.dt.from_np(a.dtype), kind="ExternalInput").ap())

    for name in _INS:
        give(f"in_{name}", inputs[name])
    n = 256
    give("consts", np.concatenate([np.eye(P), np.triu(np.ones((P, P)))], 1).astype(np.float32))
    angle = 2 * np.pi * (np.outer(np.arange(n), np.arange(n)) % n) / n
    give("dft", np.stack([np.cos(angle), np.sin(angle), -np.cos(angle)]).astype(np.float32))
    shape = inputs['x'].shape
    args.append(nc.dram_tensor("out", shape, F32, kind="ExternalOutput").ap())
    decoder_kernel(nc, *args)
    r = run_bass_kernel_spmd(nc, [arrays], core_ids=[0])
    return r.results[0]["out"]
```

```python
from contextlib import ExitStack

import concourse.bass as bass
from concourse import mybir

ALU = mybir.AluOpType
ACT = mybir.ActivationFunctionType
F32 = mybir.dt.float32
F32R = mybir.dt.float32r
BF16 = mybir.dt.bfloat16
I32 = mybir.dt.int32
X = mybir.AxisListType.X

P = 128
EPS_LN = 1e-5
EPS_DEN = 1e-6
RSQRT_SEED = 0x5F3759DF
TERMS = [(0, 0), (0, 1), (0, 2), (1, 0), (1, 1), (2, 0)]


def decoder_kernel(nc, x, ctx, w_qkv, w_gate, w_out, W_q, b_q, W_k, b_k, W_v, b_v, W_o, b_o,
                   w_re, w_im, f_bias, consts, dft, out):
    B, T, C = x.shape
    H = 16
    D = w_gate.shape[1] // H
    HD = C // H
    NT = T // P
    NC = C // P
    PAIRS = H // 2
    V1 = D + 1
    QUERY_SCALE = float(HD) ** -0.5
    assert (T, C, D, HD) == (512, 256, 64, 16)

    with ExitStack() as stack:
        def sb(name, shape, dt=F32):
            return stack.enter_context(nc.sbuf_tensor(name, shape, dt))

        def sem(name):
            return stack.enter_context(nc.semaphore(name))

        wqk_hi, wqk_lo = (sb(n, [P, NC, 2 * H * D], F32R) for n in ("wqk_hi", "wqk_lo"))
        wvg_hi, wvg_lo = (sb(n, [P, NC, 4, 512], F32R) for n in ("wvg_hi", "wvg_lo"))
        wout_hi, wout_lo = (sb(n, [P, PAIRS, C], F32R) for n in ("wout_hi", "wout_lo"))
        wx_hi, wx_lo = (sb(n, [P, 4, NC, C], F32R) for n in ("wx_hi", "wx_lo"))
        mix_hi, mix_lo = (sb(n, [P, NC, C], F32R) for n in ("mix_hi", "mix_lo"))

        ident_mask = sb("ident_mask", [P, 2 * P])
        ident = ident_mask[:, 0:P]
        causal = ident_mask[:, P:2 * P]
        bv_rows, bo_rows, fb_rows = (sb(n, [P, C]) for n in ("bv_rows", "bo_rows", "fb_rows"))
        bq_col, bk_col, bqs_col = (sb(n, [P, NC]) for n in ("bq_col", "bk_col", "bqs_col"))

        land = sb("land", [P, NT, C])
        xw = sb("xw", [P, NT, C])
        ta_hi, ta_lo, tb_hi, tb_lo = (sb(n, [P, NC, T], F32R) for n in ("ta_hi", "ta_lo", "tb_hi", "tb_lo"))
        gates = [sb(f"gates_{n}", [P, NT, 256]) for n in range(2)]
        v1 = sb("v1", [P, 2, NT, 4, V1])
        state = sb("state", [P, NT - 1, 2, V1])
        v2 = sb("v2", [P, NT, H, 32])
        ks = sb("ks", [98, H, T], BF16)
        mv = sb("mv", [P, NT, 2])
        bn6 = sb("bn6", [P, NT, 6])
        rs_v, rs_y, rs_t = (sb(n, [P, NT]) for n in ("rs_v", "rs_y", "rs_t"))
        last_mv = sb("last_mv", [P, NT, 2])
        last_v, last_y, last_t = (sb(n, [P, NT]) for n in ("last_v", "last_y", "last_t"))
        den = sb("den", [P, 4])
        rden = sb("rden", [P, 4])
        rsum = sb("rsum", [P, NT, 4])
        rowmax = sb("rowmax", [P, 4, NT, 4])
        mrow = sb("mrow", [4, 2, T], BF16)

        ARENA = 34 * 256
        arena = sb("arena", [P, ARENA])
        at = [0]

        def take(n, dt=F32):
            a = arena[:, at[0]:at[0] + n]
            at[0] += n
            assert at[0] <= ARENA
            return a if dt is F32 else a.bitcast(dt)

        raw = [take(2048) for _ in range(4)]
        at[0] = 0
        sT = take(2 * T).rearrange("p (h t) -> p h t", h=2)
        q1 = take(2 * T).rearrange("p (s t) -> p s t", s=2)
        k1 = take(2 * T).rearrange("p (s t) -> p s t", s=2)
        at_halves = at[0]
        e_part = take(2 * T).rearrange("p (s t) -> p s t", s=2)
        r_part = take(2 * T).rearrange("p (s t) -> p s t", s=2)
        at_late = at[0]
        ktok = take(3 * P).rearrange("p (c j) -> p c j", c=3)
        og = take(NT * P).rearrange("p (t n) -> p t n", t=NT)
        at[0] = 0
        qs = take(H * T // 2, BF16).rearrange("p (h t) -> p h t", h=H)
        probs = take(2 * 4 * T).rearrange("p (s h t) -> p s h t", s=2, h=4)
        oT = take(T)
        at[0] = 0
        att_out = take(NT * C).rearrange("p (t c) -> p t c", t=NT)

        def three_parts():
            return take(3 * T // 2, BF16).rearrange("p (k t) -> p k t", k=3)

        at[0] = at_halves
        parts_k = [three_parts(), three_parts()]
        rests_k = [take(T), q1[:, 0, :]]
        assert at[0] <= at_late
        at[0] = at_late
        parts_q = [three_parts(), three_parts()]
        rests_q = [take(T), take(T)]
        parts, rests = (parts_k, parts_q), (rests_k, rests_q)

        staged_parts = nc.dram_tensor("staged_parts", [2, H, len(TERMS), HD, T], BF16).ap()

        T0, T1, PJ0, PJ1, S0, S1, OA, OB = BANKS = ["T0", "T1", "PJ0", "PJ1", "S0", "S1", "OA", "OB"]
        ps = {b: stack.enter_context(nc.psum_tensor("ps_" + b, [P, 512], F32)) for b in BANKS}
        TB, PJ, SB, OBANK, FOUR = [T0, T1], [PJ0, PJ1], [S0, S1], [OA, OB], [T0, T1, PJ0, PJ1]

        full_act = {b: sem("full_act_" + b) for b in BANKS}
        full_dve = {b: sem("full_dve_" + b) for b in [PJ0, PJ1, S0, S1, OA, OB]}
        handed = {b: sem("handed_" + b) for b in FOUR}
        evacuated = {b: sem("evacuated_" + b) for b in BANKS}
        elu_halves = sem("elu_halves")
        state_ready = sem("state_ready")
        og_ready = sem("og_ready")
        x1_ready = sem("x1_ready")
        x2_ready = sem("x2_ready")
        residual_free = sem("residual_free")
        biased = sem("biased")
        last_stats = sem("last_stats")
        pool_done = sem("pool_done")
        out_ready = sem("out_ready")
        stored = sem("stored")
        x_landed = sem("x_landed")
        ctx_landed = sem("ctx_landed")
        x_consumed = sem("x_consumed")
        ctx_consumed = sem("ctx_consumed")
        first_part = [sem("first_part_k"), sem("first_part_q")]
        parts_made = [[sem(f"part_{part}_{side}") for part in range(3)] for side in "kq"]
        parts_staged = [sem(f"parts_staged_{m}") for m in range(2)]
        stacked = [sem(f"stacked_{g}") for g in range(4)]
        mrow_first = sem("mrow_first")
        mrow_ready = sem("mrow_ready")
        mrow_landed = sem("mrow_landed")
        dve_done = sem("dve_done")
        raw_landed = [sem(f"raw_landed_{n}") for n in range(6)]
        w_hi_done = sem("w_hi_done")
        w_lo_done = sem("w_lo_done")
        consts_landed = sem("consts_landed")
        four_landed = sem("four_landed")
        spec_full = sem("spec_full")
        spec_copied = sem("spec_copied")
        mix_full = sem("mix_full")
        mix_hi_done = sem("mix_hi_done")
        filled = sem("filled")

        pieces = [
            (wqk_hi[:, :, 0:1024], wqk_lo[:, :, 0:1024]),
            (wqk_hi[:, :, 1024:2048], wqk_lo[:, :, 1024:2048]),
            (wvg_hi[:, :, :, 0:256], wvg_lo[:, :, :, 0:256]),
            (wvg_hi[:, :, :, 256:512], wvg_lo[:, :, :, 256:512]),
            (wout_hi[:], wout_lo[:]),
            (wx_hi[:], wx_lo[:]),
        ]

        def raw_view(n):
            r = raw[n % 4]
            if n < 2:
                return r.rearrange("p (k c) -> p k c", k=NC)
            if n < 4:
                return r.rearrange("p (k g c) -> p k g c", k=NC, g=4)
            if n == 4:
                return r.rearrange("p (k c) -> p k c", k=PAIRS)
            return r.rearrange("p (w k c) -> p w k c", w=4, k=NC)

        w_spec = xw[:].rearrange("p (s k) c -> p s k c", s=2)
        table = v2[:].rearrange("p a b c -> p (a b c)")[:, 0:3 * NC * C].rearrange("p (s k c) -> p s k c", s=3, k=NC)
        specT = land[:].rearrange("p (s k) c -> p s k c", s=2)

        STEPS = [(g, kt) for g in range(4) for kt in range(NT)]
        AHEAD = 28
        TURN_STEPS = {4 * g + 5: g for g in range(3)}
        VALUES_AFTER = {3: (0, 0), 7: (0, 1), 11: (0, 2), 15: (0, 3), 20: (1, 0), 24: (1, 1)}
        KEY_RING = [T0, T1, PJ0]
        QUERY_RING = [S0, S1, PJ1]
        TAIL = 10
        MAXIMA_AFTER = {16 * g + 18: g for g in range(3)}
        LAST_MAXIMA = ((64 - AHEAD) // 4, 1)

        def query_bank(i):
            return QUERY_RING[(i + (i > 50)) % 3]

        def key_bank(n, j):
            if n < TAIL:
                return KEY_RING[(4 * n + j) % 3]
            return (KEY_RING + QUERY_RING)[(4 * (n - TAIL) + j) % 6]

        def max_bank(g):
            return (OA, OB, QUERY_RING[51 % 3], query_bank(64))[g]

        block = stack.enter_context(nc.Block())

        @block.sync
        def _(sp):
            def tiles(w):
                return w.rearrange("(k p) c -> p k c", p=P)

            sources = [
                [(raw_view(0), tiles(w_qkv[:, 0:1024]))],
                [(raw_view(1), tiles(w_qkv[:, 1024:2048]))],
                [(raw[2].rearrange("p (k c) -> p k c", k=NC), tiles(w_qkv[:, 2048:3072]))],
                [(raw[3].rearrange("p (k c) -> p k c", k=NC), tiles(w_gate))],
                [(raw_view(4), tiles(w_out))],
                [(raw_view(5)[:, n], tiles(w)) for n, w in enumerate((W_q, W_k, W_v, W_o))],
            ]
            for n, loads in enumerate(sources):
                if n >= 4:
                    sp.wait_ge(w_hi_done, n - 3)
                    sp.wait_ge(w_lo_done, n - 3)
                for dst, src in loads:
                    sp.dma_start(dst, src).then_inc(raw_landed[n], 16)
                if n == 3:
                    sp.dma_start(w_spec[:, 0], tiles(w_re)).then_inc(four_landed, 16)
                    sp.dma_start(w_spec[:, 1], tiles(w_im)).then_inc(four_landed, 16)
                    sp.dma_start(table, dft.rearrange("s (k p) c -> p s k c", p=P)).then_inc(four_landed, 16)
                    sp.dma_start(ident_mask[:], consts).then_inc(consts_landed, 16)
                    for dst, src in ((bv_rows, b_v), (bo_rows, b_o), (fb_rows, f_bias)):
                        sp.dma_start(dst[:], src.partition_broadcast(P)).then_inc(consts_landed, 16)
                    for dst, src in ((bq_col, b_q), (bk_col, b_k)):
                        sp.dma_start(dst[:], src.rearrange("(m p) -> p m", p=P),
                                     allow_slow_non_contiguous=True).then_inc(consts_landed, 16)
            sp.wait_ge(mix_hi_done, 1)
            sp.dma_start(land[:], x[0].rearrange("(t p) c -> p t c", p=P)).then_inc(x_landed, 16)
            with sp.Fori(0, B) as b:
                sp.wait_ge(x_consumed, 1)
                sp.sem_inc(x_consumed, -1)
                sp.dma_start(land[:], ctx[bass.ds(b, 1)].rearrange("o (t p) c -> p (o t) c", p=P)).then_inc(ctx_landed, 16)

                sp.wait_ge(ctx_consumed, 1)
                sp.sem_inc(ctx_consumed, -1)
                sp.dma_start(land[:], x[bass.ds((b + 1) % B, 1)].rearrange("o (t p) c -> p (o t) c", p=P)).then_inc(x_landed, 16)

                def stage(side, m, part):
                    sp.wait_ge(parts_made[side][part], m + 1)
                    for n, term in enumerate(TERMS):
                        if term[side] == part:
                            sp.dma_start(staged_parts[side, 8 * m:8 * m + 8, n], parts[side][m][:, part, :]
                                         ).then_inc(parts_staged[m], 16)

                def lay_out(side, m):
                    sp.wait_ge(parts_staged[m], 96 * (side + 1))
                    for h in range(8 * m, 8 * m + 8, 4):
                        sp.dma_start((ks, qs)[side][0:96, h:h + 4, :],
                                     staged_parts[side, h:h + 4].rearrange("h n d t -> (n d) h t")
                                     ).then_inc(stacked[h // 4], 16)

                for side in range(2):
                    for part in range(3):
                        stage(side, 0, part)
                    stage(side, 1, 0)
                    lay_out(side, 0)
                    for part in (1, 2):
                        stage(side, 1, part)
                    lay_out(side, 1)
                    for s in parts_made[side]:
                        sp.sem_inc(s, -2)
                for m in range(2):
                    sp.sem_inc(parts_staged[m], -192)
                for g in range(4):
                    sp.wait_ge(mrow_ready, g + 1)
                    for part in range(2):
                        sp.dma_start(qs[96 + part:97 + part, 4 * g:4 * g + 4, :], mrow[:, part, :]).then_inc(mrow_landed, 16)
                sp.sem_inc(mrow_ready, -4)
                sp.wait_ge(out_ready, 1)
                sp.sem_inc(out_ready, -1)
                sp.dma_start(out[bass.ds(b, 1)].rearrange("o (t p) c -> p (o t) c", p=P), xw[:]).then_inc(stored, 16)

        def rsqrt_seed(eng, after, v, y, var):
            after(eng.tensor_scalar(v, var, EPS_LN, None, ALU.add))
            return eng.tensor_scalar(y.bitcast(I32), v.bitcast(I32), -0.5, float(RSQRT_SEED), ALU.mult, ALU.add)

        def parts_two_three(eng, after, side, m):
            eng.wait_ge(first_part[side], m + 1)
            three, r = parts[side][m], rests[side][m]
            after(eng.tensor_tensor(r, r, three[:, 0, :], ALU.subtract))
            after(eng.tensor_copy(three[:, 1, :], r))
            eng.sem_inc(parts_made[side][1], 1)
            eng.tensor_tensor(three[:, 2, :], r, three[:, 1, :], ALU.subtract).then_inc(parts_made[side][2], 1)
            if m == 1:
                eng.sem_inc(first_part[side], -2)

        def newton(eng, after, v, t, y, fused):
            for _n in range(3):
                after(eng.tensor_tensor(t, y, y, ALU.mult))
                if fused:
                    after(eng.scalar_tensor_tensor(t, t, -0.5, v, ALU.mult, ALU.mult))
                    after(eng.scalar_tensor_tensor(y, t, 1.5, y, ALU.add, ALU.mult))
                else:
                    after(eng.tensor_tensor(t, t, v, ALU.mult))
                    after(eng.tensor_scalar(t, t, -0.5, 1.5, ALU.mult, ALU.add))
                    after(eng.tensor_tensor(y, t, y, ALU.mult))

        @block.gpsimd
        def _(pool):
            pool.memset(v1[:], 1.0).then_inc(filled, 1)
            pool.wait_ge(filled, 1)
            pool.memset(state[:], 0.0).then_inc(filled, 1)
            pool.wait_ge(filled, 2)
            pool.memset(ks[96:98], 1.0).then_inc(filled, 1)
            pool.wait_ge(filled, 3)
            pool.wait_ge(mix_hi_done, 1)
            pool.memset(v2[:, :, :, HD + 1:32], 0.0).then_inc(filled, 1)
            pool.wait_ge(filled, 4)
            pool.memset(v2[:, :, :, 0:HD + 1], 1.0).then_inc(filled, 1)
            pool.wait_ge(consts_landed, 96)

            with pool.Fori(0, B) as _b:
                own = [0]

                def after(ins):
                    own[0] += 1
                    ins.then_inc(pool_done, 1)
                    pool.wait_ge(pool_done, own[0])

                for m in range(2):
                    parts_two_three(pool, after, 0, m)
                for n, rows in enumerate((bo_rows, fb_rows)):
                    pool.wait_ge(residual_free, n + 1)
                    pool.tensor_tensor(xw[:], xw[:], rows[:].unsqueeze(1).to_broadcast([P, NT, C]), ALU.add
                                       ).then_inc(biased, 1)
                pool.sem_inc(residual_free, -2)
                pool.wait_ge(last_stats, 1)
                pool.sem_inc(last_stats, -1)
                after(rsqrt_seed(pool, after, last_v[:], last_y[:], last_mv[:, :, 1]))
                newton(pool, after, last_v[:], last_t[:], last_y[:], fused=False)
                for t in range(NT):
                    ins = pool.tensor_scalar(xw[:, t, :], xw[:, t, :], last_mv[:, t, 0:1], last_y[:, t:t + 1],
                                             ALU.subtract, ALU.mult)
                    after(ins) if t < NT - 1 else ins.then_inc(out_ready, 1)
                pool.sem_inc(pool_done, -own[0])

        @block.tensor
        def _(pe):
            pe.wait_ge(four_landed, 48)
            COS, SIN, NCOS = range(3)
            for s, (a, b) in enumerate(((COS, SIN), (SIN, NCOS))):
                for f in range(NC):
                    for e in range(NC):
                        for part, tab in enumerate((a, b)):
                            last = pe.matmul(ps[TB[s]][:, f * C:(f + 1) * C], w_spec[:, part, e, f * P:(f + 1) * P],
                                             table[:, tab, e, :], start=(f == e == part == 0),
                                             stop=(e == part == 1), skip_group_check=True)
                last.then_inc(spec_full, 1)
            pe.wait_ge(spec_copied, 2)
            for d in range(NC):
                for s, tab in enumerate((COS, SIN)):
                    for f in range(NC):
                        last = pe.matmul(ps[PJ0][:, d * C:(d + 1) * C], specT[:, s, f, d * P:(d + 1) * P],
                                         table[:, tab, f, :], start=(d == s == f == 0), stop=(s == f == 1),
                                         skip_group_check=True)
            last.then_inc(mix_full, 1)
            for bank in BANKS:
                pe.sem_inc(evacuated[bank], 1)
            pe.wait_ge(w_lo_done, 7)
            pe.wait_ge(consts_landed, 96)
            pe.wait_ge(filled, 5)

            uses = dict.fromkeys(BANKS, 0)

            def take_back(*others):
                for s, n in others:
                    pe.wait_ge(s, n)
                    pe.sem_inc(s, -n)
                for bank in BANKS:
                    if uses[bank]:
                        pe.wait_ge(evacuated[bank], uses[bank] + (bank in PJ))
                        pe.sem_inc(evacuated[bank], -uses[bank])
                for bank in BANKS:
                    uses[bank] = 0

            def claim(bank):
                uses[bank] += 1
                pe.wait_ge(evacuated[bank], uses[bank])

            def evacuated_last(*banks):
                for bank in banks:
                    pe.wait_ge(evacuated[bank], uses[bank] + 1)

            def three(out, lhs, rhs, start, stop):
                for n, (i, j) in enumerate(((0, 0), (0, 1), (1, 0))):
                    last = pe.matmul(out, lhs[i], rhs[j], start=start and n == 0, stop=stop and n == 2,
                                     skip_group_check=True)
                return last

            def turn(src, bank, c):
                claim(bank)
                for t in range(NT):
                    last = pe.transpose(ps[bank][:, t * P:(t + 1) * P], src[:, t, c * P:(c + 1) * P], ident)
                last.then_inc(full_act[bank], 1)

            def turn_normalised(ready):
                claim(T0)
                claim(T1)
                for t in range(NT):
                    if t % 2 == 0:
                        pe.wait_ge(ready, t // 2 + 1)
                    for c in range(NC):
                        last = pe.transpose(ps[TB[c]][:, t * P:(t + 1) * P], xw[:, t, c * P:(c + 1) * P], ident)
                        if t == NT - 1:
                            last.then_inc(full_act[TB[c]], 1)
                pe.sem_inc(ready, -2)

            def project(banks, w, cols, a, parts_in=()):
                for bank in banks:
                    claim(bank)
                for c in range(NC):
                    evacuated_last(*parts_in[c:c + 1])
                    for bank, f in zip(banks, cols):
                        last = three(ps[bank][:], [w[0][:, c, f], w[1][:, c, f]], [a[0][:, c, :], a[1][:, c, :]],
                                     c == 0, c == NC - 1)
                        if c == NC - 1:
                            last.then_inc(full_act[bank], 1)

            def token_major(banks, a, w, halves=(0, 1), parts_in=()):
                for bank in banks:
                    claim(bank)
                for c in range(2):
                    evacuated_last(*parts_in[c:c + 1])
                    for bank, u in zip(banks, halves):
                        for i in range(2):
                            t = 2 * u + i
                            last = three(ps[bank][:, i * C:(i + 1) * C],
                                         [a[0][:, c, t * P:(t + 1) * P], a[1][:, c, t * P:(t + 1) * P]],
                                         [w[0][:, c, :], w[1][:, c, :]], i == 0 and c == 0, c == 1)
                        if c == 1:
                            last.then_inc(full_dve[bank], 1)

            ta, tb = (ta_hi, ta_lo), (tb_hi, tb_lo)
            wqk = (wqk_hi, wqk_lo)

            qk_use = {}

            def project_qk(p, side):
                at_col = side * H * D + p * P
                project([PJ[side]], wqk, [slice(at_col, at_col + P)], ta)
                qk_use[p, side] = uses[PJ[side]]

            def values_gate(g, t, banks=PJ):
                bank = banks[t % 2]
                claim(bank)
                for c in range(NC):
                    last = three(ps[bank][:], [ta_hi[:, c, t * P:(t + 1) * P], ta_lo[:, c, t * P:(t + 1) * P]],
                                 [wvg_hi[:, c, g, :], wvg_lo[:, c, g, :]], c == 0, c == NC - 1)
                last.then_inc(full_act[bank], 1)

            def next_x():
                pe.wait_ge(x_landed, 16)
                pe.sem_inc(x_landed, -16)
                for c in range(NC):
                    turn(land, TB[c], c)

            def next_qk():
                for side in range(2):
                    project_qk(0, side)

            def next_values():
                for t in (2, 3):
                    values_gate(1, t, TB)

            next_x()
            evacuated_last(T0, T1)
            next_qk()
            next_values()
            for g, t in VALUES_AFTER.values():
                values_gate(g, t, TB)
            take_back()

            with pe.Fori(0, B) as _b:
                def out_project(g, banks):
                    token_major(banks, tb, (wout_hi[:, 2 * g:2 * g + 2], wout_lo[:, 2 * g:2 * g + 2]))

                def turn_og(p):
                    pe.wait_ge(og_ready, p + 1)
                    claim(T1)
                    for t in range(NT):
                        last = pe.transpose(ps[T1][:, t * P:(t + 1) * P], og[:, t, :], ident)
                    last.then_inc(full_act[T1], 1)

                def attend(p, c, bank, at0):
                    o = ps[bank][:, at0:at0 + 2 * V1]
                    ch = slice(c * P, (c + 1) * P)
                    if c > 0:
                        pe.matmul(o, q1[:, p % 2, ch], state[:, c - 1].rearrange("p h v -> p (h v)"),
                                  start=False, stop=False, skip_group_check=True)
                    for h in range(2):
                        last = pe.matmul(o[:, h * V1:(h + 1) * V1], sT[:, h, ch],
                                         v1[:, (p // 2) % 2, c, 2 * (p % 2) + h, :],
                                         start=(c == 0 and h == 0), stop=True, skip_group_check=True)
                    return last

                def keys_two(m):
                    project([PJ[m]], (wx_hi[:, 1], wx_lo[:, 1]), [slice(m * P, (m + 1) * P)], ta)

                def values_two(u):
                    token_major([PJ[u]], ta, (wx_hi[:, 2], wx_lo[:, 2]), [u])

                for p in range(PAIRS):
                    if p > 0:
                        for side in range(2):
                            pe.wait_ge(evacuated[PJ[side]], qk_use[p, side] + 1)
                    claim(S0)
                    claim(S1)
                    for c in range(NT):
                        ch = slice(c * P, (c + 1) * P)
                        for h in range(2):
                            hd = slice(h * D, (h + 1) * D)
                            last = pe.matmul(ps[SB[h]][:, ch], k1[hd, p % 2, ch], q1[hd, p % 2, ch],
                                             start=True, stop=True)
                            if c == NT - 1:
                                last.then_inc(full_dve[SB[h]], 1)
                    claim(T0)
                    for c in range(NT - 1):
                        last = pe.transpose(ps[T0][:, c * P:(c + 1) * P], k1[:, p % 2, c * P:(c + 1) * P], ident)
                    last.then_inc(full_act[T0], 1)
                    last_pair = p == PAIRS - 1
                    if not last_pair:
                        project_qk(p + 1, 0)
                    else:
                        pe.wait_ge(ctx_landed, 16)
                        pe.sem_inc(ctx_landed, -16)
                        for c in range(NC):
                            turn(land, PJ[c], c)
                    claim(OB)
                    evacuated_last(T0)
                    for c in range(NT - 1):
                        for h in range(2):
                            last = pe.matmul(ps[OB][h * D:(h + 1) * D, c * V1:(c + 1) * V1], ktok[:, c, h * D:(h + 1) * D],
                                             v1[:, (p // 2) % 2, c, 2 * (p % 2) + h, :],
                                             start=(c == 0), stop=True, skip_group_check=True)
                    last.then_inc(full_dve[OB], 1)
                    if not last_pair:
                        project_qk(p + 1, 1)
                    if p >= 1:
                        turn_og(p - 1)
                    g_next = p // 2 + 1
                    if 2 <= g_next < 4:
                        values_gate(g_next, 2 * (p % 2))
                    if last_pair:
                        evacuated_last(PJ0, PJ1)
                        pe.sem_inc(ctx_consumed, 1)
                        keys_two(0)
                    claim(OA)
                    evacuated_last(S0, S1)
                    attend(p, 0, OA, 0)
                    pe.wait_ge(state_ready, p + 1)
                    attend(p, 1, OA, 2 * V1).then_inc(full_dve[OA], 1)
                    if 2 <= g_next < 4:
                        values_gate(g_next, 2 * (p % 2) + 1)
                    if last_pair:
                        keys_two(1)
                    attend(p, 2, OB, 3 * V1)
                    attend(p, 3, OB, 5 * V1).then_inc(full_dve[OB], 1)
                    if p >= 2 and p % 2 == 0:
                        evacuated_last(T1)
                        out_project(p // 2 - 1, PJ)
                        if p == 2:
                            evacuated_last(PJ0, PJ1)
                            pe.sem_inc(x_consumed, 1)

                values_two(0)
                turn_og(PAIRS - 1)
                values_two(1)
                evacuated_last(T1)
                out_project(3, SB)

                turn_normalised(x1_ready)
                project(PJ, (wx_hi[:, 0], wx_lo[:, 0]), [slice(0, P), slice(P, C)], tb, TB)
                pe.sem_inc(residual_free, 1)
                next_x()

                def scores_by_query(i):
                    h, t = divmod(i, NT)
                    if i % 16 == 0:
                        pe.wait_ge(stacked[i // 16], 32)
                        pe.sem_inc(stacked[i // 16], -32)
                    bank = query_bank(i)
                    claim(bank)
                    pe.matmul(ps[bank][:], qs[0:96, h, t * P:(t + 1) * P], ks[0:96, h, :],
                              start=True, stop=True).then_inc(full_dve[bank], 1)

                def max_rows(g):
                    bank = max_bank(g)
                    claim(bank)
                    for t in range(NT):
                        last = pe.transpose(ps[bank][0:4, t * P:(t + 1) * P], rowmax[:, g, t, :], ident)
                    last.then_inc(full_act[bank], 1)

                def query_unit(i):
                    scores_by_query(i)
                    if i in MAXIMA_AFTER:
                        max_rows(MAXIMA_AFTER[i])

                probs_use = {}

                def scores_by_key(n, j):
                    g, kt = STEPS[n]
                    bank = key_bank(n, j)
                    claim(bank)
                    probs_use[n] = bank, uses[bank]
                    pe.matmul(ps[bank][:], ks[0:98, 4 * g + j, kt * P:(kt + 1) * P], qs[0:98, 4 * g + j, :],
                              start=True, stop=True).then_inc(full_act[bank], 1)

                def weigh(n):
                    g, kt = STEPS[n]
                    bank, use = probs_use[n]
                    pe.wait_ge(evacuated[bank], use + 1)
                    bank = OBANK[g % 2]
                    if kt == 0:
                        claim(bank)
                    for j in range(4):
                        last = pe.matmul(ps[bank][32 * j:32 * j + 32, :], v2[:, kt, 4 * g + j, :],
                                         probs[:, kt % 2, j, :], start=(kt == 0), stop=(kt == NT - 1),
                                         skip_group_check=True)
                    if kt == NT - 1:
                        last.then_inc(full_dve[bank], 1)

                def turn_back(g):
                    bank = OBANK[g % 2]
                    evacuated_last(bank)
                    claim(bank)
                    for t in range(NT):
                        last = pe.transpose(ps[bank][:, t * P:(t + 1) * P], oT[:, t * P:(t + 1) * P], ident)
                    last.then_inc(full_dve[bank], 1)

                for i in range(AHEAD):
                    query_unit(i)
                    if i in VALUES_AFTER:
                        values_gate(*VALUES_AFTER[i], TB)
                for n, (g, kt) in enumerate(STEPS):
                    if kt == 0:
                        pe.wait_ge(mrow_landed, 32 * (g + 1))
                    for j in range(4):
                        scores_by_key(n, j)
                        if AHEAD + 4 * n + j < 64:
                            query_unit(AHEAD + 4 * n + j)
                        if (n, j) == LAST_MAXIMA:
                            evacuated_last(*QUERY_RING)
                            max_rows(3)
                        if j == (1 if n < TAIL else 3) and n > 0:
                            weigh(n - 1)
                    if n in TURN_STEPS:
                        turn_back(TURN_STEPS[n])
                pe.sem_inc(mrow_landed, -128)
                weigh(len(STEPS) - 1)
                project_qk(0, 0)
                turn_back(3)
                project_qk(0, 1)
                evacuated_last(OB)
                for c in range(NC):
                    turn(att_out, TB[c], c)
                token_major(SB, tb, (wx_hi[:, 3], wx_lo[:, 3]), parts_in=TB)
                next_values()

                turn_normalised(x2_ready)
                token_major(OBANK, tb, (mix_hi, mix_lo), parts_in=TB)
                pe.sem_inc(residual_free, 1)
                take_back((state_ready, PAIRS), (og_ready, PAIRS))

        @block.scalar
        def _(act):
            for n, (hi, _lo) in enumerate(pieces):
                act.wait_ge(raw_landed[n], 64 if n == 5 else 16)
                act.activation(hi, raw_view(n), ACT.Copy).then_inc(w_hi_done, 1)
            for s in range(2):
                act.wait_ge(spec_full, s + 1)
                act.activation(specT[:, s].rearrange("p k c -> p (k c)"), ps[TB[s]][:], ACT.Copy).then_inc(spec_copied, 1)
            act.wait_ge(mix_full, 1)
            act.activation(mix_hi[:].rearrange("p k c -> p (k c)"), ps[PJ0][:], ACT.Copy, scale=1.0 / C).then_inc(mix_hi_done, 1)
            act.wait_ge(consts_landed, 96)
            act.activation(bqs_col[:], bq_col[:], ACT.Copy, scale=QUERY_SCALE)
            act.wait_ge(filled, 5)

            seen = dict.fromkeys(full_act, 0)

            def take_back():
                for bank in full_act:
                    if seen[bank]:
                        act.sem_inc(full_act[bank], -seen[bank])
                    seen[bank] = 0

            def full(bank):
                seen[bank] += 1
                act.wait_ge(full_act[bank], seen[bank])

            def high(bank, hi):
                full(bank)
                act.activation(hi, ps[bank][:], ACT.Copy).then_inc(handed[bank], 1)

            def elu(side):
                full(PJ[side])
                act.activation(e_part[:, side, :], ps[PJ[side]][:], ACT.Exp)
                act.activation(r_part[:, side, :], ps[PJ[side]][:], ACT.Relu).then_inc(elu_halves, 1)

            def values_gate(g, t, banks=PJ):
                bank = banks[t % 2]
                full(bank)
                act.activation(v1[:, g % 2, t, :, 0:D], ps[bank][:, 0:256].rearrange("p (h d) -> p h d", h=4), ACT.Copy)
                act.activation(gates[g % 2][:, t, :], ps[bank][:, 256:512], ACT.Tanh, scale=0.5).then_inc(evacuated[bank], 1)

            def next_x():
                for c in range(NC):
                    high(TB[c], ta_hi[:, c, :])

            def next_qk():
                for side in range(2):
                    elu(side)

            def next_values():
                for t in (2, 3):
                    values_gate(1, t, TB)

            def first_of_three(side, m):
                full(PJ[m])
                bias = (bk_col, bqs_col)[side][:, m:m + 1]
                scale = (1.0, QUERY_SCALE)[side]
                act.activation(parts[side][m][:, 0, :], ps[PJ[m]][:], ACT.Identity, bias=bias, scale=scale).then_inc(parts_made[side][0], 1)
                act.activation(rests[side][m], ps[PJ[m]][:], ACT.Identity, bias=bias, scale=scale).then_inc(first_part[side], 1)
                act.drain().then_inc(evacuated[PJ[m]], 1)

            def max_rows(g):
                full(max_bank(g))
                act.activation(mrow[:, 0, :], ps[max_bank(g)][0:4, :], ACT.Copy, scale=-1.0).then_inc(mrow_first, 1)

            next_x()
            next_qk()
            next_values()
            for g, t in VALUES_AFTER.values():
                values_gate(g, t, TB)
            take_back()
            with act.Fori(0, B) as _b:
                for p in range(PAIRS):
                    full(T0)
                    act.activation(ktok.rearrange("p c j -> p (c j)"), ps[T0][:, 0:3 * P], ACT.Copy).then_inc(evacuated[T0], 1)
                    if p + 1 < PAIRS:
                        elu(0)
                        elu(1)
                    else:
                        for c in range(NC):
                            high(PJ[c], ta_hi[:, c, :])
                    if p >= 1:
                        high(T1, tb_hi[:, (p - 1) % 2, :])
                    if 2 <= p // 2 + 1 < 4:
                        for i in range(2):
                            values_gate(p // 2 + 1, 2 * (p % 2) + i)
                for m in range(2):
                    first_of_three(0, m)
                high(T1, tb_hi[:, 1, :])
                for c in range(NC):
                    high(TB[c], tb_hi[:, c, :])
                for m in range(2):
                    first_of_three(1, m)
                next_x()

                for i in range(AHEAD):
                    if i in MAXIMA_AFTER:
                        max_rows(MAXIMA_AFTER[i])
                    if i in VALUES_AFTER:
                        values_gate(*VALUES_AFTER[i], TB)
                for n in range(16):
                    for j in range(4):
                        bank = key_bank(n, j)
                        full(bank)
                        act.activation(probs[:, n % 2, j, :], ps[bank][:], ACT.Exp).then_inc(evacuated[bank], 1)
                        i = AHEAD + 4 * n + j
                        if i in MAXIMA_AFTER:
                            max_rows(MAXIMA_AFTER[i])
                        if (n, j) == LAST_MAXIMA:
                            max_rows(3)
                next_qk()
                for c in range(NC):
                    high(TB[c], tb_hi[:, c, :])
                next_values()
                for c in range(NC):
                    high(TB[c], tb_hi[:, c, :])
                take_back()

        @block.vector
        def _(dve):
            for n, (hi, lo) in enumerate(pieces):
                dve.wait_ge(w_hi_done, n + 1)
                dve.tensor_tensor(lo, raw_view(n), hi.bitcast(F32), ALU.subtract).then_inc(w_lo_done, 1)
            dve.wait_ge(mix_hi_done, 1)
            dve.scalar_tensor_tensor(mix_lo[:].rearrange("p k c -> p (k c)"), ps[PJ0][:], 1.0 / C,
                                     mix_hi[:].rearrange("p k c -> p (k c)").bitcast(F32), ALU.mult, ALU.subtract
                                     ).then_inc(w_lo_done, 1)
            dve.sem_inc(stored, 16)
            dve.wait_ge(consts_landed, 96)
            dve.wait_ge(filled, 5)

            seen = dict.fromkeys([*full_dve, *(("handed", b) for b in handed), "elu", "mrow"], 0)
            own = [0]

            def take_back():
                for s, n in [(full_dve[b], seen[b]) for b in full_dve] + [(handed[b], seen["handed", b]) for b in handed] + [
                        (elu_halves, seen["elu"]), (mrow_first, seen["mrow"]),
                        (dve_done, own[0])]:
                    if n:
                        dve.sem_inc(s, -n)
                for key in seen:
                    seen[key] = 0
                own[0] = 0

            def after(ins):
                own[0] += 1
                ins.then_inc(dve_done, 1)
                dve.wait_ge(dve_done, own[0])

            def full(bank):
                seen[bank] += 1
                dve.wait_ge(full_dve[bank], seen[bank])

            def low(bank, hi, lo):
                seen["handed", bank] += 1
                dve.wait_ge(handed[bank], seen["handed", bank])
                dve.tensor_tensor(lo, ps[bank][:], hi.bitcast(F32), ALU.subtract).then_inc(evacuated[bank], 1)

            def elu(dst, side):
                seen["elu"] += 1
                dve.wait_ge(elu_halves, seen["elu"])
                dve.scalar_tensor_tensor(dst, e_part[:, side, :], 1.0, r_part[:, side, :], ALU.min, ALU.add
                                         ).then_inc(evacuated[PJ[side]], 1)

            def next_x():
                for c in range(NC):
                    low(TB[c], ta_hi[:, c, :], ta_lo[:, c, :])

            def next_qk():
                elu(q1[:, 0, :], 0)
                elu(k1[:, 0, :], 1)

            next_x()
            next_qk()
            take_back()
            with dve.Fori(0, B) as _b:
                def gated(p, half, bank, at0):
                    full(bank)
                    o = ps[bank][:, at0:at0 + 4 * V1].rearrange("p (n v) -> p n v", n=4)
                    after(dve.tensor_scalar(den[:], o[:, :, D], 2.0, 2.0 * EPS_DEN, ALU.mult, ALU.add))
                    after(dve.reciprocal(rden[:], den[:]))
                    dst = og[:, 2 * half:2 * half + 2, :]
                    after(dve.tensor_tensor(dst.rearrange("p c (h d) -> p (c h) d", h=2), o[:, :, 0:D],
                                            rden[:].unsqueeze(2).to_broadcast([P, 4, D]), ALU.mult))
                    gt = gates[(p // 2) % 2][:, 2 * half:2 * half + 2, (p % 2) * P:(p % 2 + 1) * P]
                    return dve.scalar_tensor_tensor(dst, gt, 1.0, dst, ALU.add, ALU.mult)

                def add_projected(u, bank, base):
                    full(bank)
                    return dve.tensor_tensor(xw[:, 2 * u:2 * u + 2, :], ps[bank][:].rearrange("p (t c) -> p t c", t=2),
                                             base[:, 2 * u:2 * u + 2, :], ALU.add)

                def add_and_measure(banks, stats):
                    for u in range(2):
                        after(add_projected(u, banks[u], xw))
                        dve.sem_inc(evacuated[banks[u]], 1)
                        for t in (2 * u, 2 * u + 1):
                            ins = dve.bn_stats(bn6[:, t, :], xw[:, t, :])
                    after(ins)
                    for t in range(NT):
                        ins = dve.bn_aggr(stats[:, t, :], bn6[:, t, :])
                    return ins

                def layer_norm(banks, ready):
                    after(add_and_measure(banks, mv))
                    after(rsqrt_seed(dve, after, rs_v[:], rs_y[:], mv[:, :, 1]))
                    newton(dve, after, rs_v[:], rs_t[:], rs_y[:], fused=True)
                    for t in range(NT):
                        ins = dve.tensor_scalar(xw[:, t, :], xw[:, t, :], mv[:, t, 0:1], rs_y[:, t:t + 1],
                                                ALU.subtract, ALU.mult)
                        if t % 2 == 1:
                            ins.then_inc(ready, 1)

                for p in range(PAIRS):
                    for h in range(2):
                        full(SB[h])
                        dve.tensor_tensor(sT[:, h, :].rearrange("p (c t) -> p c t", c=NT),
                                          ps[SB[h]][:].rearrange("p (c t) -> p c t", c=NT),
                                          causal.unsqueeze(1).to_broadcast([P, NT, P]), ALU.mult
                                          ).then_inc(evacuated[SB[h]], 1)
                    full(OB)
                    for c in range(NT - 1):
                        for h in range(2):
                            hd = slice(h * D, (h + 1) * D)
                            src = ps[OB][hd, c * V1:(c + 1) * V1]
                            if c == 0:
                                ins = dve.tensor_copy(state[hd, c, h, :], src)
                            else:
                                ins = dve.tensor_tensor(state[hd, c, h, :], src, state[hd, c - 1, h, :], ALU.add)
                        if c < NT - 2:
                            after(ins)
                    ins.then_inc(state_ready, 1)
                    if p + 1 < PAIRS:
                        elu(q1[:, (p + 1) % 2, :], 0)
                        elu(k1[:, (p + 1) % 2, :], 1)
                    else:
                        for c in range(NC):
                            low(PJ[c], ta_hi[:, c, :], ta_lo[:, c, :])
                    if p >= 1:
                        low(T1, tb_hi[:, (p - 1) % 2, :], tb_lo[:, (p - 1) % 2, :])
                    gated(p, 0, OA, 0).then_inc(evacuated[OA], 1)
                    gated(p, 1, OB, 3 * V1).then_inc(og_ready, 1)
                    dve.drain().then_inc(evacuated[OB], 1)
                    if p >= 2 and p % 2 == 0:
                        if p == 2:
                            dve.wait_ge(stored, 16)
                            dve.sem_inc(stored, -16)
                        for u in range(2):
                            add_projected(u, PJ[u], land if p == 2 else xw).then_inc(evacuated[PJ[u]], 1)
                low(T1, tb_hi[:, 1, :], tb_lo[:, 1, :])
                for u in range(2):
                    full(PJ[u])
                    for i in range(2):
                        ins = dve.tensor_tensor(v2[:, 2 * u + i, :, 0:HD],
                                                ps[PJ[u]][:, i * C:(i + 1) * C].rearrange("p (h d) -> p h d", h=H),
                                                bv_rows[:].rearrange("p (h d) -> p h d", h=H), ALU.add)
                    ins.then_inc(evacuated[PJ[u]], 1)
                layer_norm(SB, x1_ready)
                for c in range(NC):
                    low(TB[c], tb_hi[:, c, :], tb_lo[:, c, :])
                for m in range(2):
                    parts_two_three(dve, after, 1, m)
                next_x()

                def row_max(i):
                    h, t = divmod(i, NT)
                    bank = query_bank(i)
                    dst = rowmax[:, h // 4, t, h % 4:h % 4 + 1]
                    full(bank)
                    dve.tensor_reduce(dst, ps[bank][:], X, ALU.max).then_inc(evacuated[bank], 1)

                def max_rows(g):
                    seen["mrow"] += 1
                    dve.wait_ge(mrow_first, seen["mrow"])
                    dve.scalar_tensor_tensor(mrow[:, 1, :], ps[max_bank(g)][0:4, :], -1.0, mrow[:, 0, :],
                                             ALU.mult, ALU.subtract).then_inc(mrow_ready, 1)
                    dve.drain().then_inc(evacuated[max_bank(g)], 1)

                def keep_sums(g):
                    bank = OBANK[g % 2]
                    full(bank)
                    dve.tensor_copy(oT, ps[bank][:]).then_inc(evacuated[bank], 1)

                def normalise(g):
                    bank = OBANK[g % 2]
                    full(bank)
                    o = ps[bank][:].rearrange("p (t h d) -> p t h d", t=NT, h=4)
                    after(dve.reciprocal(rsum[:], o[:, :, :, HD]))
                    dst = att_out[:, :, g * 4 * HD:(g + 1) * 4 * HD].rearrange("p t (h d) -> p t h d", h=4)
                    dve.tensor_tensor(dst, o[:, :, :, 0:HD], rsum[:].unsqueeze(3).to_broadcast([P, NT, 4, HD]), ALU.mult
                                      ).then_inc(evacuated[bank], 1)

                def query_unit(i):
                    row_max(i)
                    if i - 2 in MAXIMA_AFTER:
                        max_rows(MAXIMA_AFTER[i - 2])

                for i in range(AHEAD):
                    query_unit(i)
                for n in range(16):
                    for j in range(4):
                        if AHEAD + 4 * n + j < 64:
                            query_unit(AHEAD + 4 * n + j)
                        if (n, j) == LAST_MAXIMA:
                            max_rows(3)
                        if j == 1 and n - 1 in TURN_STEPS:
                            normalise(TURN_STEPS[n - 1])
                    if n + 1 in TURN_STEPS:
                        keep_sums(TURN_STEPS[n + 1])
                keep_sums(3)
                normalise(3)
                for c in range(NC):
                    low(TB[c], tb_hi[:, c, :], tb_lo[:, c, :])
                dve.wait_ge(biased, 1)
                layer_norm(SB, x2_ready)
                next_qk()
                for c in range(NC):
                    low(TB[c], tb_hi[:, c, :], tb_lo[:, c, :])
                dve.wait_ge(biased, 2)
                dve.sem_inc(biased, -2)
                add_and_measure(OBANK, last_mv).then_inc(last_stats, 1)
                take_back()
            dve.wait_ge(stored, 16)


_INS = ['x', 'ctx_1024', 'L0_attn_w_qkv', 'L0_attn_w_gate', 'L0_attn_w_out', 'L0_xattn_W_q', 'L0_xattn_b_q',
        'L0_xattn_W_k', 'L0_xattn_b_k', 'L0_xattn_W_v', 'L0_xattn_b_v', 'L0_xattn_W_o', 'L0_xattn_b_o',
        'L0_ffn_w_freq_real', 'L0_ffn_w_freq_imag', 'L0_ffn_bias']


def kernel(**inputs):
    import numpy as np
    import concourse.bacc as bacc
    from concourse.bass_utils import run_bass_kernel_spmd

    nc = bacc.Bacc("TRN2", target_bir_lowering=False, num_devices=1)
    arrays, args = {}, []

    def give(name, a):
        a = np.ascontiguousarray(a)
        arrays[name] = a
        args.append(nc.dram_tensor(name, a.shape, mybir.dt.from_np(a.dtype), kind="ExternalInput").ap())

    for name in _INS:
        give(f"in_{name}", inputs[name])
    n = 256
    give("consts", np.concatenate([np.eye(P), np.triu(np.ones((P, P)))], 1).astype(np.float32))
    angle = 2 * np.pi * (np.outer(np.arange(n), np.arange(n)) % n) / n
    give("dft", np.stack([np.cos(angle), np.sin(angle), -np.cos(angle)]).astype(np.float32))
    shape = inputs['x'].shape
    args.append(nc.dram_tensor("out", shape, F32, kind="ExternalOutput").ap())
    decoder_kernel(nc, *args)
    r = run_bass_kernel_spmd(nc, [arrays], core_ids=[0])
    return r.results[0]["out"]
```

```python
from contextlib import ExitStack

import concourse.bass as bass
from concourse import mybir

ALU = mybir.AluOpType
ACT = mybir.ActivationFunctionType
F32 = mybir.dt.float32
F32R = mybir.dt.float32r
BF16 = mybir.dt.bfloat16
I32 = mybir.dt.int32
X = mybir.AxisListType.X

P = 128
EPS_LN = 1e-5
EPS_DEN = 1e-6
RSQRT_SEED = 0x5F3759DF
TERMS = [(0, 0), (0, 1), (0, 2), (1, 0), (1, 1), (2, 0)]


def decoder_kernel(nc, x, ctx, w_qkv, w_gate, w_out, W_q, b_q, W_k, b_k, W_v, b_v, W_o, b_o,
                   w_re, w_im, f_bias, consts, dft, out):
    B, T, C = x.shape
    H = 16
    D = w_gate.shape[1] // H
    HD = C // H
    NT = T // P
    NC = C // P
    PAIRS = H // 2
    V1 = D + 1
    QUERY_SCALE = float(HD) ** -0.5
    assert (T, C, D, HD) == (512, 256, 64, 16)

    with ExitStack() as stack:
        def sb(name, shape, dt=F32):
            return stack.enter_context(nc.sbuf_tensor(name, shape, dt))

        def sem(name):
            return stack.enter_context(nc.semaphore(name))

        wqk_hi, wqk_lo = (sb(n, [P, NC, 2 * H * D], F32R) for n in ("wqk_hi", "wqk_lo"))
        wvg_hi, wvg_lo = (sb(n, [P, NC, 4, 512], F32R) for n in ("wvg_hi", "wvg_lo"))
        wout_hi, wout_lo = (sb(n, [P, PAIRS, C], F32R) for n in ("wout_hi", "wout_lo"))
        wx_hi, wx_lo = (sb(n, [P, 4, NC, C], F32R) for n in ("wx_hi", "wx_lo"))
        mix_hi, mix_lo = (sb(n, [P, NC, C], F32R) for n in ("mix_hi", "mix_lo"))

        ident_mask = sb("ident_mask", [P, 2 * P])
        ident = ident_mask[:, 0:P]
        causal = ident_mask[:, P:2 * P]
        bv_rows, bo_rows, fb_rows = (sb(n, [P, C]) for n in ("bv_rows", "bo_rows", "fb_rows"))
        bq_col, bk_col, bqs_col = (sb(n, [P, NC]) for n in ("bq_col", "bk_col", "bqs_col"))

        land = sb("land", [P, NT, C])
        xw = sb("xw", [P, NT, C])
        ta_hi, ta_lo, tb_hi, tb_lo = (sb(n, [P, NC, T], F32R) for n in ("ta_hi", "ta_lo", "tb_hi", "tb_lo"))
        gates = [sb(f"gates_{n}", [P, NT, 256]) for n in range(2)]
        v1 = sb("v1", [P, 2, NT, 4, V1])
        state = sb("state", [P, NT - 1, 2, V1])
        v2 = sb("v2", [P, NT, H, 32])
        ks = sb("ks", [98, H, T], BF16)
        mv = sb("mv", [P, NT, 2])
        bn6 = sb("bn6", [P, NT, 6])
        rs_v, rs_y, rs_t = (sb(n, [P, NT]) for n in ("rs_v", "rs_y", "rs_t"))
        last_mv = sb("last_mv", [P, NT, 2])
        last_v, last_y, last_t = (sb(n, [P, NT]) for n in ("last_v", "last_y", "last_t"))
        den = sb("den", [P, 4])
        rden = sb("rden", [P, 4])
        rsum = sb("rsum", [P, NT, 4])
        rowmax = sb("rowmax", [P, 4, NT, 4])
        mrow = sb("mrow", [4, 2, T], BF16)

        ARENA = 34 * 256
        arena = sb("arena", [P, ARENA])
        at = [0]

        def take(n, dt=F32):
            a = arena[:, at[0]:at[0] + n]
            at[0] += n
            assert at[0] <= ARENA
            return a if dt is F32 else a.bitcast(dt)

        raw = [take(2048) for _ in range(4)]
        at[0] = 0
        sT = take(2 * T).rearrange("p (h t) -> p h t", h=2)
        q1 = take(2 * T).rearrange("p (s t) -> p s t", s=2)
        k1 = take(2 * T).rearrange("p (s t) -> p s t", s=2)
        at_halves = at[0]
        e_part = take(2 * T).rearrange("p (s t) -> p s t", s=2)
        r_part = take(2 * T).rearrange("p (s t) -> p s t", s=2)
        at_late = at[0]
        ktok = take(3 * P).rearrange("p (c j) -> p c j", c=3)
        og = take(NT * P).rearrange("p (t n) -> p t n", t=NT)
        at[0] = 0
        qs = take(H * T // 2, BF16).rearrange("p (h t) -> p h t", h=H)
        at_probs = at[0]
        probs = take(2 * 4 * T).rearrange("p (s h t) -> p s h t", s=2, h=4)
        oT = take(T)
        at[0] = 0
        att_out = take(NT * C).rearrange("p (t c) -> p t c", t=NT)

        def three_parts():
            return take(3 * T // 2, BF16).rearrange("p (k t) -> p k t", k=3)

        at[0] = at_halves
        parts_k = [three_parts()]
        at[0] = at_probs
        parts_k.append(three_parts())
        assert at[0] <= at_late
        at[0] = at_late
        parts_q = [three_parts(), three_parts()]
        rests_q = [take(T), take(T)]
        rests_k = [take(T), take(T)]
        parts, rests = (parts_k, parts_q), (rests_k, rests_q)

        staged_parts = nc.dram_tensor("staged_parts", [2, H, len(TERMS), HD, T], BF16).ap()

        T0, T1, PJ0, PJ1, S0, S1, OA, OB = BANKS = ["T0", "T1", "PJ0", "PJ1", "S0", "S1", "OA", "OB"]
        ps = {b: stack.enter_context(nc.psum_tensor("ps_" + b, [P, 512], F32)) for b in BANKS}
        TB, PJ, SB, OBANK, FOUR = [T0, T1], [PJ0, PJ1], [S0, S1], [OA, OB], [T0, T1, PJ0, PJ1]

        full_act = {b: sem("full_act_" + b) for b in BANKS}
        full_dve = {b: sem("full_dve_" + b) for b in BANKS}
        handed = {b: sem("handed_" + b) for b in [*FOUR, OA, OB]}
        evacuated = {b: sem("evacuated_" + b) for b in BANKS}
        elu_halves = sem("elu_halves")
        state_ready = sem("state_ready")
        og_ready = sem("og_ready")
        x1_ready = sem("x1_ready")
        x2_ready = sem("x2_ready")
        residual_free = sem("residual_free")
        biased = sem("biased")
        last_stats = sem("last_stats")
        pool_done = sem("pool_done")
        out_ready = sem("out_ready")
        stored = sem("stored")
        x_landed = sem("x_landed")
        ctx_landed = sem("ctx_landed")
        x_consumed = sem("x_consumed")
        ctx_consumed = sem("ctx_consumed")
        first_part = [sem("first_part_k"), sem("first_part_q")]
        parts_made = [[sem(f"part_{part}_{side}") for part in range(3)] for side in "kq"]
        parts_staged = [sem(f"parts_staged_{m}") for m in range(2)]
        keys_stacked = [sem(f"keys_stacked_{m}") for m in range(2)]
        queries_stacked = [sem(f"queries_stacked_{n}") for n in range(4)]
        mrow_first = sem("mrow_first")
        mrow_ready = sem("mrow_ready")
        mrow_landed = sem("mrow_landed")
        dve_done = sem("dve_done")
        raw_landed = [sem(f"raw_landed_{n}") for n in range(6)]
        w_hi_done = sem("w_hi_done")
        w_lo_done = sem("w_lo_done")
        ident_landed = sem("ident_landed")
        consts_landed = sem("consts_landed")
        four_landed = sem("four_landed")
        spec_full = sem("spec_full")
        spec_copied = sem("spec_copied")
        mix_full = sem("mix_full")
        mix_hi_done = sem("mix_hi_done")
        filled = sem("filled")

        pieces = [
            (wvg_hi[:, :, :, 0:256], wvg_lo[:, :, :, 0:256]),
            (wvg_hi[:, :, :, 256:512], wvg_lo[:, :, :, 256:512]),
            (wqk_hi[:, :, 0:1024], wqk_lo[:, :, 0:1024]),
            (wqk_hi[:, :, 1024:2048], wqk_lo[:, :, 1024:2048]),
            (wout_hi[:], wout_lo[:]),
            (wx_hi[:], wx_lo[:]),
        ]

        def raw_view(n):
            r = raw[n % 4]
            if n < 2:
                return r.rearrange("p (k g c) -> p k g c", k=NC, g=4)
            if n < 4:
                return r.rearrange("p (k c) -> p k c", k=NC)
            if n == 4:
                return r.rearrange("p (k c) -> p k c", k=PAIRS)
            return r.rearrange("p (w k c) -> p w k c", w=4, k=NC)

        w_spec = xw[:].rearrange("p (s k) c -> p s k c", s=2)
        table = v2[:].rearrange("p a b c -> p (a b c)")[:, 0:3 * NC * C].rearrange("p (s k c) -> p s k c", s=3, k=NC)
        specT = raw[2][:, 0:NT * C].rearrange("p (s k c) -> p s k c", s=2, k=NC)

        STEPS = [(g, kt) for g in range(4) for kt in range(NT)]
        AHEAD = 28
        TURN_STEPS = {4 * g + 6: g for g in range(3)}
        VALUES_AFTER = {-4: (0, 0), -3: (0, 1), -2: (0, 2), -1: (0, 3), 20: (1, 0), 24: (1, 1)}
        KEY_RING = [T0, T1, PJ0]
        QUERY_RING = [S0, S1, PJ1]
        TAIL = 10
        MAXIMA_AFTER = {16 * g + 18: g for g in range(3)}
        LAST_MAXIMA = ((64 - AHEAD) // 4, 1)

        def query_bank(i):
            return QUERY_RING[i % 3]

        def key_bank(n, j):
            if n < TAIL:
                return KEY_RING[(4 * n + j) % 3]
            return (KEY_RING + QUERY_RING)[(4 * (n - TAIL) + j) % 6]

        def max_bank(g):
            return (OA, OB, OA, query_bank(64))[g]

        block = stack.enter_context(nc.Block())

        @block.sync
        def _(sp):
            def tiles(w):
                return w.rearrange("(k p) c -> p k c", p=P)

            sources = [
                [(raw[0].rearrange("p (k c) -> p k c", k=NC), tiles(w_qkv[:, 2048:3072]))],
                [(raw[1].rearrange("p (k c) -> p k c", k=NC), tiles(w_gate))],
                [(raw_view(2), tiles(w_qkv[:, 0:1024]))],
                [(raw_view(3), tiles(w_qkv[:, 1024:2048]))],
                [(raw_view(4), tiles(w_out))],
                [(raw_view(5)[:, n], tiles(w)) for n, w in enumerate((W_q, W_k, W_v, W_o))],
            ]
            sp.dma_start(ident_mask[:], consts).then_inc(ident_landed, 16)
            sp.dma_start(land[:], x[0].rearrange("(t p) c -> p t c", p=P)).then_inc(x_landed, 16)
            for n, loads in enumerate(sources):
                if n >= 4:
                    sp.wait_ge(w_hi_done, n - 3)
                    sp.wait_ge(w_lo_done, n - 3)
                for dst, src in loads:
                    sp.dma_start(dst, src).then_inc(raw_landed[n], 16)
                if n == 3:
                    sp.dma_start(w_spec[:, 0], tiles(w_re)).then_inc(four_landed, 16)
                    sp.dma_start(w_spec[:, 1], tiles(w_im)).then_inc(four_landed, 16)
                    sp.dma_start(table, dft.rearrange("s (k p) c -> p s k c", p=P)).then_inc(four_landed, 16)
                    for dst, src in ((bv_rows, b_v), (bo_rows, b_o), (fb_rows, f_bias)):
                        sp.dma_start(dst[:], src.partition_broadcast(P)).then_inc(consts_landed, 16)
                    for dst, src in ((bq_col, b_q), (bk_col, b_k)):
                        sp.dma_start(dst[:], src.rearrange("(m p) -> p m", p=P),
                                     allow_slow_non_contiguous=True).then_inc(consts_landed, 16)
            with sp.Fori(0, B) as b:
                sp.wait_ge(x_consumed, 1)
                sp.sem_inc(x_consumed, -1)
                sp.dma_start(land[:], ctx[bass.ds(b, 1)].rearrange("o (t p) c -> p (o t) c", p=P)).then_inc(ctx_landed, 16)

                sp.wait_ge(ctx_consumed, 1)
                sp.sem_inc(ctx_consumed, -1)
                sp.dma_start(land[:], x[bass.ds((b + 1) % B, 1)].rearrange("o (t p) c -> p (o t) c", p=P)).then_inc(x_landed, 16)

                def stage(side, m, part):
                    sp.wait_ge(parts_made[side][part], m + 1)
                    for n, term in enumerate(TERMS):
                        if term[side] == part:
                            sp.dma_start(staged_parts[side, 8 * m:8 * m + 8, n], parts[side][m][:, part, :]
                                         ).then_inc(parts_staged[m], 16)

                def lay_out(side, h0, h1, done):
                    sp.dma_start((ks, qs)[side][0:96, h0:h1, :],
                                 staged_parts[side, h0:h1].rearrange("h n d t -> (n d) h t")).then_inc(done, 16)

                def stage_all(side, m):
                    for part in range(3):
                        stage(side, m, part)

                def wait_staged(side, m):
                    sp.wait_ge(parts_staged[m], 96 * (side + 1))

                stage_all(0, 0)
                wait_staged(0, 0)
                lay_out(0, 0, 8, keys_stacked[0])
                stage_all(1, 0)
                wait_staged(1, 0)
                lay_out(1, 0, 2, queries_stacked[0])
                lay_out(1, 2, 4, queries_stacked[1])
                lay_out(1, 4, 8, queries_stacked[2])
                stage_all(0, 1)
                wait_staged(0, 1)
                lay_out(0, 8, 16, keys_stacked[1])
                stage_all(1, 1)
                wait_staged(1, 1)
                lay_out(1, 8, 16, queries_stacked[3])
                for side in range(2):
                    for s in parts_made[side]:
                        sp.sem_inc(s, -2)
                for m in range(2):
                    sp.sem_inc(parts_staged[m], -192)
                for g in range(4):
                    sp.wait_ge(mrow_ready, g + 1)
                    for part in range(2):
                        sp.dma_start(qs[96 + part:97 + part, 4 * g:4 * g + 4, :], mrow[:, part, :]).then_inc(mrow_landed, 16)
                sp.sem_inc(mrow_ready, -4)
                sp.wait_ge(out_ready, 1)
                sp.sem_inc(out_ready, -1)
                sp.dma_start(out[bass.ds(b, 1)].rearrange("o (t p) c -> p (o t) c", p=P), xw[:]).then_inc(stored, 16)

        def rsqrt_seed(eng, after, v, y, var):
            after(eng.tensor_scalar(v, var, EPS_LN, None, ALU.add))
            return eng.tensor_scalar(y.bitcast(I32), v.bitcast(I32), -0.5, float(RSQRT_SEED), ALU.mult, ALU.add)

        def parts_two_three(eng, after, side, m):
            eng.wait_ge(first_part[side], m + 1)
            three, r = parts[side][m], rests[side][m]
            after(eng.tensor_tensor(r, r, three[:, 0, :], ALU.subtract))
            after(eng.tensor_copy(three[:, 1, :], r))
            eng.sem_inc(parts_made[side][1], 1)
            eng.tensor_tensor(three[:, 2, :], r, three[:, 1, :], ALU.subtract).then_inc(parts_made[side][2], 1)
            if m == 1:
                eng.sem_inc(first_part[side], -2)

        def newton(eng, after, v, t, y, fused):
            for _n in range(3):
                after(eng.tensor_tensor(t, y, y, ALU.mult))
                if fused:
                    after(eng.scalar_tensor_tensor(t, t, -0.5, v, ALU.mult, ALU.mult))
                    after(eng.scalar_tensor_tensor(y, t, 1.5, y, ALU.add, ALU.mult))
                else:
                    after(eng.tensor_tensor(t, t, v, ALU.mult))
                    after(eng.tensor_scalar(t, t, -0.5, 1.5, ALU.mult, ALU.add))
                    after(eng.tensor_tensor(y, t, y, ALU.mult))

        @block.gpsimd
        def _(pool):
            pool.memset(v1[:], 1.0).then_inc(filled, 1)
            pool.wait_ge(filled, 1)
            pool.memset(state[:], 0.0).then_inc(filled, 1)
            pool.wait_ge(filled, 2)
            pool.memset(ks[96:98], 1.0).then_inc(filled, 1)
            pool.wait_ge(filled, 3)
            pool.wait_ge(mix_hi_done, 1)
            pool.memset(v2[:, :, :, HD + 1:32], 0.0).then_inc(filled, 1)
            pool.wait_ge(filled, 4)
            pool.memset(v2[:, :, :, 0:HD + 1], 1.0).then_inc(filled, 1)
            pool.wait_ge(consts_landed, 80)

            with pool.Fori(0, B) as _b:
                own = [0]

                def after(ins):
                    own[0] += 1
                    ins.then_inc(pool_done, 1)
                    pool.wait_ge(pool_done, own[0])

                for m in range(2):
                    parts_two_three(pool, after, 0, m)
                for n, rows in enumerate((bo_rows, fb_rows)):
                    pool.wait_ge(residual_free, n + 1)
                    pool.tensor_tensor(xw[:], xw[:], rows[:].unsqueeze(1).to_broadcast([P, NT, C]), ALU.add
                                       ).then_inc(biased, 1)
                pool.sem_inc(residual_free, -2)
                pool.wait_ge(last_stats, 1)
                pool.sem_inc(last_stats, -1)
                after(rsqrt_seed(pool, after, last_v[:], last_y[:], last_mv[:, :, 1]))
                newton(pool, after, last_v[:], last_t[:], last_y[:], fused=False)
                for t in range(NT):
                    ins = pool.tensor_scalar(xw[:, t, :], xw[:, t, :], last_mv[:, t, 0:1], last_y[:, t:t + 1],
                                             ALU.subtract, ALU.mult)
                    after(ins) if t < NT - 1 else ins.then_inc(out_ready, 1)
                pool.sem_inc(pool_done, -own[0])

        @block.tensor
        def _(pe):
            uses = dict.fromkeys(BANKS, 0)

            def take_back(*others):
                for s, n in others:
                    pe.wait_ge(s, n)
                    pe.sem_inc(s, -n)
                for bank in BANKS:
                    if uses[bank]:
                        pe.wait_ge(evacuated[bank], uses[bank])
                        pe.sem_inc(evacuated[bank], -uses[bank])
                for bank in BANKS:
                    uses[bank] = 0

            def claim(bank):
                uses[bank] += 1
                pe.wait_ge(evacuated[bank], uses[bank])

            def evacuated_last(*banks):
                for bank in banks:
                    pe.wait_ge(evacuated[bank], uses[bank] + 1)

            def three(out, lhs, rhs, start, stop):
                for n, (i, j) in enumerate(((0, 0), (0, 1), (1, 0))):
                    last = pe.matmul(out, lhs[i], rhs[j], start=start and n == 0, stop=stop and n == 2,
                                     skip_group_check=True)
                return last

            def turn(src, bank, c):
                claim(bank)
                for t in range(NT):
                    last = pe.transpose(ps[bank][:, t * P:(t + 1) * P], src[:, t, c * P:(c + 1) * P], ident)
                last.then_inc(full_act[bank], 1)

            def turn_halves(src, ready=None):
                for u in range(2):
                    claim(TB[u])
                    if ready is not None:
                        pe.wait_ge(ready, u + 1)
                    for c in range(NC):
                        for t in (2 * u, 2 * u + 1):
                            at_col = c * C + (t % 2) * P
                            last = pe.transpose(ps[TB[u]][:, at_col:at_col + P], src[:, t, c * P:(c + 1) * P], ident)
                    last.then_inc(full_act[TB[u]], 1)
                if ready is not None:
                    pe.sem_inc(ready, -2)

            def project(banks, w, cols, a):
                for bank, f in zip(banks, cols):
                    claim(bank)
                    for c in range(NC):
                        last = three(ps[bank][:], [w[0][:, c, f], w[1][:, c, f]], [a[0][:, c, :], a[1][:, c, :]],
                                     c == 0, c == NC - 1)
                    last.then_inc(full_act[bank], 1)

            def project_halves(banks, w, cols, a):
                for bank in banks:
                    claim(bank)
                for u in range(2):
                    half = slice(u * C, (u + 1) * C)
                    evacuated_last(TB[u])
                    for bank, f in zip(banks, cols):
                        for c in range(NC):
                            last = three(ps[bank][:, half], [w[0][:, c, f], w[1][:, c, f]],
                                         [a[0][:, c, half], a[1][:, c, half]], u == 0 and c == 0, c == NC - 1)
                        if u == 1:
                            last.then_inc(full_act[bank], 1)

            def token_major(banks, a, w, halves=(0, 1), comes_by_halves=False):
                for bank, u in zip(banks, halves):
                    if comes_by_halves:
                        evacuated_last(TB[u])
                    claim(bank)
                    for i in range(2):
                        t = 2 * u + i
                        for c in range(2):
                            last = three(ps[bank][:, i * C:(i + 1) * C],
                                         [a[0][:, c, t * P:(t + 1) * P], a[1][:, c, t * P:(t + 1) * P]],
                                         [w[0][:, c, :], w[1][:, c, :]], i == 0 and c == 0, c == 1)
                    last.then_inc(full_dve[bank], 1)

            ta, tb = (ta_hi, ta_lo), (tb_hi, tb_lo)
            wqk = (wqk_hi, wqk_lo)

            qk_use = {}

            def project_qk(p, side):
                at_col = side * H * D + p * P
                project([PJ[side]], wqk, [slice(at_col, at_col + P)], ta)
                qk_use[p, side] = uses[PJ[side]]

            def values_gate(g, t, banks=PJ):
                bank = banks[t % 2]
                claim(bank)
                for c in range(NC):
                    last = three(ps[bank][:], [ta_hi[:, c, t * P:(t + 1) * P], ta_lo[:, c, t * P:(t + 1) * P]],
                                 [wvg_hi[:, c, g, :], wvg_lo[:, c, g, :]], c == 0, c == NC - 1)
                last.then_inc(full_act[bank], 1)

            def pair_scores(p):
                claim(S0)
                claim(S1)
                for c in range(NT):
                    ch = slice(c * P, (c + 1) * P)
                    for h in range(2):
                        hd = slice(h * D, (h + 1) * D)
                        last = pe.matmul(ps[SB[h]][:, ch], k1[hd, p % 2, ch], q1[hd, p % 2, ch],
                                         start=True, stop=True)
                        if c == NT - 1:
                            last.then_inc(full_dve[SB[h]], 1)
                claim(T0)
                for c in range(NT - 1):
                    last = pe.transpose(ps[T0][:, c * P:(c + 1) * P], k1[:, p % 2, c * P:(c + 1) * P], ident)
                last.then_inc(full_act[T0], 1)

            def contributions(p):
                claim(OB)
                evacuated_last(T0)
                for c in range(NT - 1):
                    for h in range(2):
                        last = pe.matmul(ps[OB][h * D:(h + 1) * D, c * V1:(c + 1) * V1], ktok[:, c, h * D:(h + 1) * D],
                                         v1[:, (p // 2) % 2, c, 2 * (p % 2) + h, :],
                                         start=(c == 0), stop=True, skip_group_check=True)
                last.then_inc(full_dve[OB], 1)

            def next_x(banks):
                pe.wait_ge(x_landed, 16)
                pe.sem_inc(x_landed, -16)
                for c in range(NC):
                    turn(land, banks[c], c)

            def next_qk():
                for side in range(2):
                    project_qk(0, side)

            def next_values():
                for t in (2, 3):
                    values_gate(1, t, TB)

            for bank in BANKS:
                pe.sem_inc(evacuated[bank], 1)
            pe.wait_ge(ident_landed, 16)
            next_x(PJ)
            evacuated_last(*PJ)
            pe.wait_ge(w_lo_done, 2)
            next_values()
            for g, t in VALUES_AFTER.values():
                values_gate(g, t, TB)

            pe.wait_ge(four_landed, 48)
            COS, SIN, NCOS = range(3)
            for s, (a, b) in enumerate(((COS, SIN), (SIN, NCOS))):
                for f in range(NC):
                    for e in range(NC):
                        for part, tab in enumerate((a, b)):
                            last = pe.matmul(ps[OBANK[s]][:, f * C:(f + 1) * C], w_spec[:, part, e, f * P:(f + 1) * P],
                                             table[:, tab, e, :], start=(f == e == part == 0),
                                             stop=(e == part == 1), skip_group_check=True)
                last.then_inc(spec_full, 1)
            pe.wait_ge(spec_copied, 2)
            for d in range(NC):
                for s, tab in enumerate((COS, SIN)):
                    for f in range(NC):
                        last = pe.matmul(ps[S0][:, d * C:(d + 1) * C], specT[:, s, f, d * P:(d + 1) * P],
                                         table[:, tab, f, :], start=(d == s == f == 0), stop=(s == f == 1),
                                         skip_group_check=True)
            last.then_inc(mix_full, 1)
            pe.wait_ge(w_lo_done, 7)
            pe.wait_ge(filled, 5)
            next_qk()
            evacuated_last(*PJ)
            pair_scores(0)
            contributions(0)
            take_back()

            with pe.Fori(0, B) as _b:
                def out_project(g, banks):
                    token_major(banks, tb, (wout_hi[:, 2 * g:2 * g + 2], wout_lo[:, 2 * g:2 * g + 2]))

                def turn_og(p):
                    pe.wait_ge(og_ready, p + 1)
                    claim(T1)
                    for t in range(NT):
                        last = pe.transpose(ps[T1][:, t * P:(t + 1) * P], og[:, t, :], ident)
                    last.then_inc(full_act[T1], 1)

                def attend(p, c, bank, at0):
                    o = ps[bank][:, at0:at0 + 2 * V1]
                    ch = slice(c * P, (c + 1) * P)
                    if c > 0:
                        pe.matmul(o, q1[:, p % 2, ch], state[:, c - 1].rearrange("p h v -> p (h v)"),
                                  start=False, stop=False, skip_group_check=True)
                    for h in range(2):
                        last = pe.matmul(o[:, h * V1:(h + 1) * V1], sT[:, h, ch],
                                         v1[:, (p // 2) % 2, c, 2 * (p % 2) + h, :],
                                         start=(c == 0 and h == 0), stop=True, skip_group_check=True)
                    return last

                def keys_two(m):
                    project([PJ[m]], (wx_hi[:, 1], wx_lo[:, 1]), [slice(m * P, (m + 1) * P)], ta)

                def values_two(u, bank):
                    token_major([bank], ta, (wx_hi[:, 2], wx_lo[:, 2]), [u])

                for p in range(PAIRS):
                    if p > 0:
                        for side in range(2):
                            pe.wait_ge(evacuated[PJ[side]], qk_use[p, side] + 1)
                        pair_scores(p)
                    last_pair = p == PAIRS - 1
                    if not last_pair:
                        project_qk(p + 1, 0)
                    else:
                        pe.wait_ge(ctx_landed, 16)
                        pe.sem_inc(ctx_landed, -16)
                        for c in range(NC):
                            turn(land, PJ[c], c)
                    if p > 0:
                        contributions(p)
                    if not last_pair:
                        project_qk(p + 1, 1)
                    if p == 3:
                        pe.sem_inc(x_consumed, 1)
                    if p >= 1:
                        turn_og(p - 1)
                    g_next = p // 2 + 1
                    if 2 <= g_next < 4:
                        values_gate(g_next, 2 * (p % 2))
                    claim(OA)
                    evacuated_last(S0, S1)
                    attend(p, 0, OA, 0)
                    pe.wait_ge(state_ready, p + 1)
                    attend(p, 1, OA, 2 * V1).then_inc(full_dve[OA], 1)
                    if 2 <= g_next < 4:
                        values_gate(g_next, 2 * (p % 2) + 1)
                    attend(p, 2, OB, 3 * V1)
                    attend(p, 3, OB, 5 * V1).then_inc(full_dve[OB], 1)
                    if p >= 2 and p % 2 == 0:
                        evacuated_last(T1)
                        out_project(p // 2 - 1, PJ)

                evacuated_last(PJ0, PJ1)
                pe.sem_inc(ctx_consumed, 1)
                values_two(0, PJ0)
                turn_og(PAIRS - 1)
                evacuated_last(T1)
                out_project(3, SB)
                for m in range(2):
                    keys_two(m)
                values_two(1, S0)
                next_x(OBANK)

                turn_halves(xw, x1_ready)
                project_halves(PJ, (wx_hi[:, 0], wx_lo[:, 0]), [slice(0, P), slice(P, C)], tb)
                pe.sem_inc(residual_free, 1)

                def scores_by_query(i):
                    h, t = divmod(i, NT)
                    if i % 32 == 0:
                        pe.wait_ge(keys_stacked[i // 32], 16)
                        pe.sem_inc(keys_stacked[i // 32], -16)
                    if h in (0, 2, 4, 8) and t == 0:
                        n = (0, 2, 4, 8).index(h)
                        pe.wait_ge(queries_stacked[n], 16)
                        pe.sem_inc(queries_stacked[n], -16)
                    bank = query_bank(i)
                    claim(bank)
                    pe.matmul(ps[bank][:], qs[0:96, h, t * P:(t + 1) * P], ks[0:96, h, :],
                              start=True, stop=True).then_inc(full_dve[bank], 1)

                def max_rows(g):
                    bank = max_bank(g)
                    claim(bank)
                    for t in range(NT):
                        last = pe.transpose(ps[bank][0:4, t * P:(t + 1) * P], rowmax[:, g, t, :], ident)
                    last.then_inc(full_act[bank], 1)

                def query_unit(i):
                    scores_by_query(i)
                    if i in MAXIMA_AFTER:
                        max_rows(MAXIMA_AFTER[i])

                probs_use = {}

                def scores_by_key(n, j):
                    g, kt = STEPS[n]
                    bank = key_bank(n, j)
                    claim(bank)
                    probs_use[n] = bank, uses[bank]
                    pe.matmul(ps[bank][:], ks[0:98, 4 * g + j, kt * P:(kt + 1) * P], qs[0:98, 4 * g + j, :],
                              start=True, stop=True).then_inc(full_act[bank], 1)

                def weigh(n):
                    g, kt = STEPS[n]
                    bank, use = probs_use[n]
                    pe.wait_ge(evacuated[bank], use + 1)
                    bank = OBANK[g % 2]
                    if kt == 0:
                        claim(bank)
                    for j in range(4):
                        last = pe.matmul(ps[bank][32 * j:32 * j + 32, :], v2[:, kt, 4 * g + j, :],
                                         probs[:, kt % 2, j, :], start=(kt == 0), stop=(kt == NT - 1),
                                         skip_group_check=True)
                    if kt == NT - 1:
                        last.then_inc(full_dve[bank], 1)

                def turn_back(g):
                    bank = OBANK[g % 2]
                    evacuated_last(bank)
                    claim(bank)
                    for t in range(NT):
                        last = pe.transpose(ps[bank][:, t * P:(t + 1) * P], oT[:, t * P:(t + 1) * P], ident)
                    last.then_inc(full_dve[bank], 1)

                evacuated_last(*OBANK)
                for i in range(-4, AHEAD):
                    if i >= 0:
                        query_unit(i)
                    if i in VALUES_AFTER:
                        values_gate(*VALUES_AFTER[i], TB)
                for n, (g, kt) in enumerate(STEPS):
                    if kt == 0:
                        pe.wait_ge(mrow_landed, 32 * (g + 1))
                    for j in range(4):
                        scores_by_key(n, j)
                        if AHEAD + 4 * n + j < 64:
                            query_unit(AHEAD + 4 * n + j)
                        if (n, j) == LAST_MAXIMA:
                            evacuated_last(*QUERY_RING)
                            max_rows(3)
                        if j == (1 if n < TAIL else 3) and n > 0:
                            weigh(n - 1)
                    if n in TURN_STEPS:
                        turn_back(TURN_STEPS[n])
                pe.sem_inc(mrow_landed, -128)
                weigh(len(STEPS) - 1)
                project_qk(0, 0)
                turn_back(3)
                project_qk(0, 1)
                evacuated_last(OB)
                turn_halves(att_out)
                token_major(SB, tb, (wx_hi[:, 3], wx_lo[:, 3]), comes_by_halves=True)
                next_values()
                evacuated_last(*PJ)
                pair_scores(0)
                contributions(0)

                turn_halves(xw, x2_ready)
                token_major(TB, tb, (mix_hi, mix_lo), comes_by_halves=True)
                pe.sem_inc(residual_free, 1)
                take_back((state_ready, PAIRS), (og_ready, PAIRS))

        @block.scalar
        def _(act):
            seen = dict.fromkeys(full_act, 0)

            def take_back():
                for bank in full_act:
                    if seen[bank]:
                        act.sem_inc(full_act[bank], -seen[bank])
                    seen[bank] = 0

            def full(bank):
                seen[bank] += 1
                act.wait_ge(full_act[bank], seen[bank])

            def high(bank, hi):
                full(bank)
                act.activation(hi, ps[bank][:], ACT.Copy).then_inc(handed[bank], 1)

            def elu(side):
                full(PJ[side])
                act.activation(e_part[:, side, :], ps[PJ[side]][:], ACT.Exp)
                act.activation(r_part[:, side, :], ps[PJ[side]][:], ACT.Relu).then_inc(elu_halves, 1)

            def values_gate(g, t, banks=PJ):
                bank = banks[t % 2]
                full(bank)
                act.activation(v1[:, g % 2, t, :, 0:D], ps[bank][:, 0:256].rearrange("p (h d) -> p h d", h=4), ACT.Copy)
                act.activation(gates[g % 2][:, t, :], ps[bank][:, 256:512], ACT.Tanh, scale=0.5).then_inc(evacuated[bank], 1)

            def high_halves():
                for u in range(2):
                    full(TB[u])
                    act.activation(tb_hi[:, :, u * C:(u + 1) * C], ps[TB[u]][:].rearrange("p (c t) -> p c t", c=NC), ACT.Copy
                                   ).then_inc(handed[TB[u]], 1)

            def next_x(banks):
                for c in range(NC):
                    high(banks[c], ta_hi[:, c, :])

            def keys_by_token():
                full(T0)
                act.activation(ktok.rearrange("p c j -> p (c j)"), ps[T0][:, 0:3 * P], ACT.Copy).then_inc(evacuated[T0], 1)

            def next_qk():
                for side in range(2):
                    elu(side)

            def next_values():
                for t in (2, 3):
                    values_gate(1, t, TB)

            def first_of_three(side, m):
                full(PJ[m])
                bias = (bk_col, bqs_col)[side][:, m:m + 1]
                scale = (1.0, QUERY_SCALE)[side]
                act.activation(parts[side][m][:, 0, :], ps[PJ[m]][:], ACT.Identity, bias=bias, scale=scale).then_inc(parts_made[side][0], 1)
                act.activation(rests[side][m], ps[PJ[m]][:], ACT.Identity, bias=bias, scale=scale).then_inc(first_part[side], 1)
                act.drain().then_inc(evacuated[PJ[m]], 1)

            def max_rows(g):
                full(max_bank(g))
                act.activation(mrow[:, 0, :], ps[max_bank(g)][0:4, :], ACT.Copy, scale=-1.0).then_inc(mrow_first, 1)

            def split(n):
                act.wait_ge(raw_landed[n], 64 if n == 5 else 16)
                act.activation(pieces[n][0], raw_view(n), ACT.Copy).then_inc(w_hi_done, 1)

            next_x(PJ)
            split(0)
            split(1)
            act.wait_ge(filled, 1)
            split(2)
            next_values()
            split(3)
            for g, t in list(VALUES_AFTER.values())[:3]:
                values_gate(g, t, TB)
            split(4)
            for g, t in list(VALUES_AFTER.values())[3:]:
                values_gate(g, t, TB)
            split(5)
            act.wait_ge(w_lo_done, 3)
            for s in range(2):
                act.wait_ge(spec_full, s + 1)
                act.activation(specT[:, s].rearrange("p k c -> p (k c)"), ps[OBANK[s]][:], ACT.Copy).then_inc(spec_copied, 1)
            act.wait_ge(mix_full, 1)
            act.activation(mix_hi[:].rearrange("p k c -> p (k c)"), ps[S0][:], ACT.Copy, scale=1.0 / C).then_inc(mix_hi_done, 1)
            act.wait_ge(consts_landed, 80)
            act.activation(bqs_col[:], bq_col[:], ACT.Copy, scale=QUERY_SCALE)
            act.wait_ge(filled, 5)
            next_qk()
            keys_by_token()
            take_back()
            with act.Fori(0, B) as _b:
                for p in range(PAIRS):
                    if p > 0:
                        keys_by_token()
                    if p + 1 < PAIRS:
                        elu(0)
                        elu(1)
                    else:
                        for c in range(NC):
                            high(PJ[c], ta_hi[:, c, :])
                    if p >= 1:
                        high(T1, tb_hi[:, (p - 1) % 2, :])
                    if 2 <= p // 2 + 1 < 4:
                        for i in range(2):
                            values_gate(p // 2 + 1, 2 * (p % 2) + i)
                high(T1, tb_hi[:, 1, :])
                for m in range(2):
                    first_of_three(0, m)
                next_x(OBANK)
                high_halves()
                for m in range(2):
                    first_of_three(1, m)

                for i in range(-4, AHEAD):
                    if i in MAXIMA_AFTER:
                        max_rows(MAXIMA_AFTER[i])
                    if i in VALUES_AFTER:
                        values_gate(*VALUES_AFTER[i], TB)
                for n in range(16):
                    for j in range(4):
                        bank = key_bank(n, j)
                        full(bank)
                        act.activation(probs[:, n % 2, j, :], ps[bank][:], ACT.Exp).then_inc(evacuated[bank], 1)
                        i = AHEAD + 4 * n + j
                        if i in MAXIMA_AFTER:
                            max_rows(MAXIMA_AFTER[i])
                        if (n, j) == LAST_MAXIMA:
                            max_rows(3)
                next_qk()
                high_halves()
                next_values()
                keys_by_token()
                high_halves()
                take_back()

        @block.vector
        def _(dve):
            seen = dict.fromkeys([*full_dve, *(("handed", b) for b in handed), "elu", "mrow"], 0)
            own = [0]

            def take_back():
                for s, n in [(full_dve[b], seen[b]) for b in full_dve] + [(handed[b], seen["handed", b]) for b in handed] + [
                        (elu_halves, seen["elu"]), (mrow_first, seen["mrow"]),
                        (dve_done, own[0])]:
                    if n:
                        dve.sem_inc(s, -n)
                for key in seen:
                    seen[key] = 0
                own[0] = 0

            def after(ins):
                own[0] += 1
                ins.then_inc(dve_done, 1)
                dve.wait_ge(dve_done, own[0])

            def full(bank):
                seen[bank] += 1
                dve.wait_ge(full_dve[bank], seen[bank])

            def low(bank, hi, lo):
                seen["handed", bank] += 1
                dve.wait_ge(handed[bank], seen["handed", bank])
                dve.tensor_tensor(lo, ps[bank][:], hi.bitcast(F32), ALU.subtract).then_inc(evacuated[bank], 1)

            def elu(dst, side):
                seen["elu"] += 1
                dve.wait_ge(elu_halves, seen["elu"])
                dve.scalar_tensor_tensor(dst, e_part[:, side, :], 1.0, r_part[:, side, :], ALU.min, ALU.add
                                         ).then_inc(evacuated[PJ[side]], 1)

            def low_halves():
                for u in range(2):
                    half = slice(u * C, (u + 1) * C)
                    seen["handed", TB[u]] += 1
                    dve.wait_ge(handed[TB[u]], seen["handed", TB[u]])
                    dve.tensor_tensor(tb_lo[:, :, half], ps[TB[u]][:].rearrange("p (c t) -> p c t", c=NC),
                                      tb_hi[:, :, half].bitcast(F32), ALU.subtract).then_inc(evacuated[TB[u]], 1)

            def next_x(banks):
                for c in range(NC):
                    low(banks[c], ta_hi[:, c, :], ta_lo[:, c, :])

            def sum_states():
                full(OB)
                for c in range(NT - 1):
                    for h in range(2):
                        hd = slice(h * D, (h + 1) * D)
                        src = ps[OB][hd, c * V1:(c + 1) * V1]
                        if c == 0:
                            ins = dve.tensor_copy(state[hd, c, h, :], src)
                        else:
                            ins = dve.tensor_tensor(state[hd, c, h, :], src, state[hd, c - 1, h, :], ALU.add)
                    if c < NT - 2:
                        after(ins)
                ins.then_inc(state_ready, 1)

            def mask():
                for h in range(2):
                    full(SB[h])
                    dve.tensor_tensor(sT[:, h, :].rearrange("p (c t) -> p c t", c=NT),
                                      ps[SB[h]][:].rearrange("p (c t) -> p c t", c=NT),
                                      causal.unsqueeze(1).to_broadcast([P, NT, P]), ALU.mult
                                      ).then_inc(evacuated[SB[h]], 1)

            def next_qk():
                elu(q1[:, 0, :], 0)
                elu(k1[:, 0, :], 1)

            next_x(PJ)
            for n, (hi, lo) in enumerate(pieces):
                dve.wait_ge(w_hi_done, n + 1)
                dve.tensor_tensor(lo, raw_view(n), hi.bitcast(F32), ALU.subtract).then_inc(w_lo_done, 1)
            dve.wait_ge(mix_hi_done, 1)
            dve.scalar_tensor_tensor(mix_lo[:].rearrange("p k c -> p (k c)"), ps[S0][:], 1.0 / C,
                                     mix_hi[:].rearrange("p k c -> p (k c)").bitcast(F32), ALU.mult, ALU.subtract
                                     ).then_inc(w_lo_done, 1)
            dve.sem_inc(stored, 16)
            dve.wait_ge(consts_landed, 80)
            dve.wait_ge(filled, 5)
            next_qk()
            mask()
            sum_states()
            take_back()
            with dve.Fori(0, B) as _b:
                def gated(p, half, bank, at0):
                    full(bank)
                    o = ps[bank][:, at0:at0 + 4 * V1].rearrange("p (n v) -> p n v", n=4)
                    after(dve.tensor_scalar(den[:], o[:, :, D], 2.0, 2.0 * EPS_DEN, ALU.mult, ALU.add))
                    after(dve.reciprocal(rden[:], den[:]))
                    dst = og[:, 2 * half:2 * half + 2, :]
                    after(dve.tensor_tensor(dst.rearrange("p c (h d) -> p (c h) d", h=2), o[:, :, 0:D],
                                            rden[:].unsqueeze(2).to_broadcast([P, 4, D]), ALU.mult))
                    gt = gates[(p // 2) % 2][:, 2 * half:2 * half + 2, (p % 2) * P:(p % 2 + 1) * P]
                    return dve.scalar_tensor_tensor(dst, gt, 1.0, dst, ALU.add, ALU.mult)

                def add_projected(u, bank, base):
                    full(bank)
                    return dve.tensor_tensor(xw[:, 2 * u:2 * u + 2, :], ps[bank][:].rearrange("p (t c) -> p t c", t=2),
                                             base[:, 2 * u:2 * u + 2, :], ALU.add)

                def add_and_measure(banks, stats):
                    for u in range(2):
                        after(add_projected(u, banks[u], xw))
                        dve.sem_inc(evacuated[banks[u]], 1)
                        for t in (2 * u, 2 * u + 1):
                            ins = dve.bn_stats(bn6[:, t, :], xw[:, t, :])
                    after(ins)
                    for t in range(NT):
                        ins = dve.bn_aggr(stats[:, t, :], bn6[:, t, :])
                    return ins

                def layer_norm(banks, ready):
                    after(add_and_measure(banks, mv))
                    after(rsqrt_seed(dve, after, rs_v[:], rs_y[:], mv[:, :, 1]))
                    newton(dve, after, rs_v[:], rs_t[:], rs_y[:], fused=True)
                    for t in range(NT):
                        ins = dve.tensor_scalar(xw[:, t, :], xw[:, t, :], mv[:, t, 0:1], rs_y[:, t:t + 1],
                                                ALU.subtract, ALU.mult)
                        if t % 2 == 1:
                            ins.then_inc(ready, 1)

                for p in range(PAIRS):
                    if p > 0:
                        mask()
                        sum_states()
                    if p + 1 < PAIRS:
                        elu(q1[:, (p + 1) % 2, :], 0)
                        elu(k1[:, (p + 1) % 2, :], 1)
                    else:
                        for c in range(NC):
                            low(PJ[c], ta_hi[:, c, :], ta_lo[:, c, :])
                    if p >= 1:
                        low(T1, tb_hi[:, (p - 1) % 2, :], tb_lo[:, (p - 1) % 2, :])
                    gated(p, 0, OA, 0).then_inc(evacuated[OA], 1)
                    gated(p, 1, OB, 3 * V1).then_inc(og_ready, 1)
                    dve.drain().then_inc(evacuated[OB], 1)
                    if p >= 2 and p % 2 == 0:
                        if p == 2:
                            dve.wait_ge(stored, 16)
                            dve.sem_inc(stored, -16)
                        for u in range(2):
                            add_projected(u, PJ[u], land if p == 2 else xw).then_inc(evacuated[PJ[u]], 1)
                low(T1, tb_hi[:, 1, :], tb_lo[:, 1, :])
                def values_two(u, bank):
                    full(bank)
                    for i in range(2):
                        ins = dve.tensor_tensor(v2[:, 2 * u + i, :, 0:HD],
                                                ps[bank][:, i * C:(i + 1) * C].rearrange("p (h d) -> p h d", h=H),
                                                bv_rows[:].rearrange("p (h d) -> p h d", h=H), ALU.add)
                    ins.then_inc(evacuated[bank], 1)

                values_two(0, PJ0)
                layer_norm(SB, x1_ready)
                low_halves()
                next_x(OBANK)
                values_two(1, S0)
                for m in range(2):
                    parts_two_three(dve, after, 1, m)

                def row_max(i):
                    h, t = divmod(i, NT)
                    bank = query_bank(i)
                    dst = rowmax[:, h // 4, t, h % 4:h % 4 + 1]
                    full(bank)
                    dve.tensor_reduce(dst, ps[bank][:], X, ALU.max).then_inc(evacuated[bank], 1)

                def max_rows(g):
                    seen["mrow"] += 1
                    dve.wait_ge(mrow_first, seen["mrow"])
                    dve.scalar_tensor_tensor(mrow[:, 1, :], ps[max_bank(g)][0:4, :], -1.0, mrow[:, 0, :],
                                             ALU.mult, ALU.subtract).then_inc(mrow_ready, 1)
                    dve.drain().then_inc(evacuated[max_bank(g)], 1)

                def keep_sums(g):
                    bank = OBANK[g % 2]
                    full(bank)
                    dve.tensor_copy(oT, ps[bank][:]).then_inc(evacuated[bank], 1)

                def normalise(g):
                    bank = OBANK[g % 2]
                    full(bank)
                    o = ps[bank][:].rearrange("p (t h d) -> p t h d", t=NT, h=4)
                    after(dve.reciprocal(rsum[:], o[:, :, :, HD]))
                    dst = att_out[:, :, g * 4 * HD:(g + 1) * 4 * HD].rearrange("p t (h d) -> p t h d", h=4)
                    dve.tensor_tensor(dst, o[:, :, :, 0:HD], rsum[:].unsqueeze(3).to_broadcast([P, NT, 4, HD]), ALU.mult
                                      ).then_inc(evacuated[bank], 1)

                def query_unit(i):
                    row_max(i)
                    if i - 2 in MAXIMA_AFTER:
                        max_rows(MAXIMA_AFTER[i - 2])

                take_back()
                for i in range(AHEAD):
                    query_unit(i)
                for n in range(16):
                    for j in range(4):
                        if AHEAD + 4 * n + j < 64:
                            query_unit(AHEAD + 4 * n + j)
                        if (n, j) == LAST_MAXIMA:
                            max_rows(3)
                        if j == 1 and n - 1 in TURN_STEPS:
                            normalise(TURN_STEPS[n - 1])
                    if n + 2 in TURN_STEPS:
                        keep_sums(TURN_STEPS[n + 2])
                keep_sums(3)
                normalise(3)
                low_halves()
                next_qk()
                dve.wait_ge(biased, 1)
                layer_norm(SB, x2_ready)
                low_halves()
                mask()
                sum_states()
                take_back()
                dve.wait_ge(biased, 2)
                dve.sem_inc(biased, -2)
                add_and_measure(TB, last_mv).then_inc(last_stats, 1)
                take_back()
            dve.wait_ge(stored, 16)


_INS = ['x', 'ctx_1024', 'L0_attn_w_qkv', 'L0_attn_w_gate', 'L0_attn_w_out', 'L0_xattn_W_q', 'L0_xattn_b_q',
        'L0_xattn_W_k', 'L0_xattn_b_k', 'L0_xattn_W_v', 'L0_xattn_b_v', 'L0_xattn_W_o', 'L0_xattn_b_o',
        'L0_ffn_w_freq_real', 'L0_ffn_w_freq_imag', 'L0_ffn_bias']


def kernel(**inputs):
    import numpy as np
    import concourse.bacc as bacc
    from concourse.bass_utils import run_bass_kernel_spmd

    nc = bacc.Bacc("TRN2", target_bir_lowering=False, num_devices=1)
    arrays, args = {}, []

    def give(name, a):
        a = np.ascontiguousarray(a)
        arrays[name] = a
        args.append(nc.dram_tensor(name, a.shape, mybir.dt.from_np(a.dtype), kind="ExternalInput").ap())

    for name in _INS:
        give(f"in_{name}", inputs[name])
    n = 256
    give("consts", np.concatenate([np.eye(P), np.triu(np.ones((P, P)))], 1).astype(np.float32))
    angle = 2 * np.pi * (np.outer(np.arange(n), np.arange(n)) % n) / n
    give("dft", np.stack([np.cos(angle), np.sin(angle), -np.cos(angle)]).astype(np.float32))
    shape = inputs['x'].shape
    args.append(nc.dram_tensor("out", shape, F32, kind="ExternalOutput").ap())
    decoder_kernel(nc, *args)
    r = run_bass_kernel_spmd(nc, [arrays], core_ids=[0])
    return r.results[0]["out"]
```
